# Optimizing a Trainium2 kernel written in Bass

```python
import numpy as np
import jax
import jax.numpy as jnp

def _softmax(x, axis=-1):
    return jax.nn.softmax(x, axis=axis)

def _gelu(x):
    return jax.nn.gelu(x, approximate=True)

def _silu(x):
    return jax.nn.silu(x)

def _sigmoid(x):
    return jax.nn.sigmoid(x)

def _layernorm(x, axis=-1, eps=1e-05):
    m = jnp.mean(x, axis=axis, keepdims=True)
    v = jnp.var(x, axis=axis, keepdims=True)
    return (x - m) / jnp.sqrt(v + eps)

def _scatter_add(tgt, idx, src, axis=0):
    return tgt.at[idx].add(src)

def _segment_sum(src, seg, n):
    return jax.ops.segment_sum(src, seg, n)
kernel_name = 'mk_prb_d1_jaxref_r8_9037d1'

def setup_inputs(seed: int=0):
    np.random.seed(seed)
    _w = jnp.asarray

    def _L0_attn_setup():
        import jax, jax.numpy as jnp
        import numpy as np
        EMBED_DIM = 128
        NUM_HEADS = 16
        HEAD_DIM = EMBED_DIM // NUM_HEADS
        BATCH = 2
        SEQ = 256
        NEG_INF = float('-inf')
        key = jax.random.key(seed)
        k1, k2, k3, k4, k5 = jax.random.split(key, 5)
        return {'query': jax.random.normal(k1, (BATCH, SEQ, EMBED_DIM), dtype=jnp.float32), 'key': jax.random.normal(k2, (BATCH, SEQ, EMBED_DIM), dtype=jnp.float32), 'value': jax.random.normal(k3, (BATCH, SEQ, EMBED_DIM), dtype=jnp.float32), 'in_proj_weight': jax.random.normal(k4, (3 * EMBED_DIM, EMBED_DIM), dtype=jnp.float32) * (1.0 / np.sqrt(EMBED_DIM)), 'out_proj_weight': jax.random.normal(k5, (EMBED_DIM, EMBED_DIM), dtype=jnp.float32) * (1.0 / np.sqrt(EMBED_DIM))}
    _L0_attn_in = _L0_attn_setup()

    def _L0_ffn_setup():
        import jax, jax.numpy as jnp
        import numpy as np
        H, I, E_ROUTED, TOP_K = (128, 352, 7, 2)
        B, S = (4, 256)

        def _expert(h, g, u, d):
            return jnp.einsum('...i,hi->...h', jax.nn.silu(h @ g.T) * (h @ u.T), d)
        key = jax.random.key(seed)
        ks = jax.random.split(key, 10)
        sc = 0.02
        return {'x': jax.random.normal(ks[0], (B, S, H), dtype=jnp.float32), 'sg': jax.random.normal(ks[1], (I, H), dtype=jnp.float32) * sc, 'su': jax.random.normal(ks[2], (I, H), dtype=jnp.float32) * sc, 'sd': jax.random.normal(ks[3], (H, I), dtype=jnp.float32) * sc, 'rg': jax.random.normal(ks[4], (E_ROUTED, I, H), dtype=jnp.float32) * sc, 'ru': jax.random.normal(ks[5], (E_ROUTED, I, H), dtype=jnp.float32) * sc, 'rd': jax.random.normal(ks[6], (E_ROUTED, H, I), dtype=jnp.float32) * sc, 'wr': jax.random.normal(ks[7], (E_ROUTED, H), dtype=jnp.float32) * sc, 'rb': jnp.zeros((E_ROUTED,), dtype=jnp.float32)}
    _L0_ffn_in = _L0_ffn_setup()
    _d = {'L0_attn_query': _L0_attn_in['query'], 'L0_attn_key': _L0_attn_in['key'], 'L0_attn_value': _L0_attn_in['value'], 'L0_attn_in_proj_weight': _L0_attn_in['in_proj_weight'], 'L0_attn_out_proj_weight': _L0_attn_in['out_proj_weight'], 'L0_ffn_sg': _L0_ffn_in['sg'], 'L0_ffn_su': _L0_ffn_in['su'], 'L0_ffn_sd': _L0_ffn_in['sd'], 'L0_ffn_rg': _L0_ffn_in['rg'], 'L0_ffn_ru': _L0_ffn_in['ru'], 'L0_ffn_rd': _L0_ffn_in['rd'], 'L0_ffn_wr': _L0_ffn_in['wr'], 'L0_ffn_rb': _L0_ffn_in['rb']}
    _x0 = _d['L0_attn_query']
    _d['L0_attn_query'] = jax.random.normal(jax.random.fold_in(jax.random.key(seed), 1), (16, 256, 128), dtype=_x0.dtype)
    del _x0
    return _d

def reference(L0_attn_query, L0_attn_key, L0_attn_value, L0_attn_in_proj_weight, L0_attn_out_proj_weight, L0_ffn_sg, L0_ffn_su, L0_ffn_sd, L0_ffn_rg, L0_ffn_ru, L0_ffn_rd, L0_ffn_wr, L0_ffn_rb):

    def _L0_attn_ref(query, key, value, in_proj_weight, out_proj_weight):
        import jax, jax.numpy as jnp
        import numpy as np
        EMBED_DIM = 128
        NUM_HEADS = 16
        HEAD_DIM = EMBED_DIM // NUM_HEADS
        BATCH = 2
        SEQ = 256
        NEG_INF = float('-inf')
        B, T, E = query.shape
        H, D = (NUM_HEADS, HEAD_DIM)
        projected = jnp.einsum('bte,fe->btf', query, in_proj_weight)
        packed = projected.reshape(B, T, 3, H, D).transpose(0, 3, 2, 1, 4)
        q, k, v = (packed[:, :, 0], packed[:, :, 1], packed[:, :, 2])
        q = q / jnp.sqrt(jnp.asarray(D, dtype=q.dtype))
        attention = jnp.einsum('bhtd,bhkd->bhtk', q, k)
        qpos = jnp.arange(T)[:, None]
        kpos = jnp.arange(T)[None, :]
        mask = jnp.where(qpos - kpos >= 0, 0.0, NEG_INF).astype(attention.dtype)
        attention = attention + mask[None, None]
        activation = jax.nn.softmax(attention, axis=-1)
        x = jnp.einsum('bhtk,bhkd->bhtd', activation, v)
        x = x.transpose(0, 2, 1, 3).reshape(B, T, E)
        out = jnp.einsum('bte,fe->btf', x, out_proj_weight)
        return out

    def _L0_ffn_ref(x, sg, su, sd, rg, ru, rd, wr, rb):
        import jax, jax.numpy as jnp
        import numpy as np
        H, I, E_ROUTED, TOP_K = (128, 352, 7, 2)
        B, S = (4, 256)

        def _expert(h, g, u, d):
            return jnp.einsum('...i,hi->...h', jax.nn.silu(h @ g.T) * (h @ u.T), d)
        shared_out = _expert(x, sg, su, sd)
        logits = x @ wr.T + rb
        probs = jax.nn.softmax(logits, axis=-1)
        scores, idx = jax.lax.top_k(probs, TOP_K)
        scores = scores / scores.sum(axis=-1, keepdims=True)
        w = jnp.sum(scores[..., None] * jax.nn.one_hot(idx, E_ROUTED, dtype=x.dtype), axis=-2)
        out = shared_out
        for e in range(E_ROUTED):
            out = out + w[..., e:e + 1] * _expert(x, rg[e], ru[e], rd[e])
        return out
    x = L0_attn_query
    xn = _layernorm(x, axis=-1)
    x = x + _L0_attn_ref(xn, L0_attn_key, L0_attn_value, L0_attn_in_proj_weight, L0_attn_out_proj_weight) + _L0_ffn_ref(xn, L0_ffn_sg, L0_ffn_su, L0_ffn_sd, L0_ffn_rg, L0_ffn_ru, L0_ffn_rd, L0_ffn_wr, L0_ffn_rb)
    return x

_drawn_inputs = setup_inputs


def setup_inputs(seed=0):
    import zlib

    import numpy as np

    out = dict(_drawn_inputs(seed))
    spreads = {'L0_ffn_rb': (0.0, 0.8)}
    factors = {'L0_ffn_sg': 5.812,
     'L0_ffn_su': 5.644,
     'L0_ffn_sd': 5.678,
     'L0_ffn_rg': 8.0,
     'L0_ffn_ru': 8.0,
     'L0_ffn_rd': 8.0,
     'L0_ffn_wr': 8.0}
    for name, (base, spread) in spreads.items():
        noise = np.random.default_rng([zlib.crc32(name.encode()), seed]).standard_normal(out[name].shape)
        drawn = base * np.exp(spread * noise) if base else spread * noise
        out[name] = jnp.asarray(drawn.astype(out[name].dtype))
    for name, factor in factors.items():
        out[name] = (out[name] * factor).astype(out[name].dtype)
    return out
```

```python
from contextlib import ExitStack

import numpy as np

import concourse.bass as bass
from concourse import mybir

F32 = mybir.dt.float32
F32R = mybir.dt.float32r
BF16 = mybir.dt.bfloat16
ALU = mybir.AluOpType
ACT = mybir.ActivationFunctionType
AX = mybir.AxisListType

NB, SEQ, EMB = 16, 256, 128
HEADS, HD = 16, 8
QUADS = 4
NQ = NB * QUADS
TILES = NB * SEQ // 128
TPC = 4
CH = TPC * 128
NC = TILES // TPC
EXP, INNER = 8, 352
ROUTED = EXP - 1
TPX = EXP * 3
ROWS = [128, 128, INNER - 256]
WE = 2 * INNER + 3 * 128
PIECE = EXP * WE // NB
N_PREP = 17
NEG = -1e30
SCALE = float(HD) ** -0.5
EPS = 1e-5
C_ID, C_MASK, C_COL, C_SEL = 0, 128, 256, 260
C_ALL = C_SEL + ROUTED * 128
S_IN, S_OUT, S_R, S_ALL = 0, 384, 512, 520


def constants():
    c = np.zeros((128, C_ALL), np.float32)
    p = np.arange(128)
    c[:, C_ID:C_ID + 128] = np.eye(128)
    c[:, C_MASK:C_MASK + 128] = np.where(p[:, None] >= p[None, :], 0.0, NEG)
    part = p % 32 // HD
    c[:, C_COL] = np.where(part == 1, -1.0, 0.0)
    c[:, C_COL + 1] = np.where(part == 2, -1.0, 0.0)
    c[(p % 32 == 24) | (p % 32 == 25), C_COL + 1] = 1.0
    c[(p % 32 == 24) | (p % 32 == 25), C_COL + 2] = 1.0
    for r in range(ROUTED):
        c[r, C_SEL + 128 * r:C_SEL + 128 * r + 128] = 1.0
        c[8 + r, C_SEL + 128 * r:C_SEL + 128 * r + 128] = 1.0
    return c


def build(nc, x_d, small_d, rb_d, w_d, const_d, out_d):
    with ExitStack() as ctx:
        def sb(name, shape, dt=F32):
            return ctx.enter_context(nc.sbuf_tensor("sb_" + name, shape, dt))

        def sem(name):
            return ctx.enter_context(nc.semaphore(name))

        x_sb = sb("x_sb", [128, TILES, 128])
        xh_all = sb("xh_all", [128, NB * SEQ], F32R)
        xl_all = sb("xl_all", [128, NB * SEQ], F32R)
        o_all = sb("o_all", [128, NB * SEQ])
        wh_all = sb("wh_all", [128, EXP * WE], F32R)
        wl_all = sb("wl_all", [128, EXP * WE], F32R)
        const = sb("const", [128, C_SEL])
        ident_r = sb("ident_r", [128, 128], F32R)
        small = sb("small", [128, S_ALL])
        small_h = sb("small_h", [128, S_ALL], F32R)
        small_l = sb("small_l", [128, S_ALL], F32R)
        sel_r = sb("sel_r", [16, ROUTED * 128], F32R)
        rb = sb("rb", [128, 8])
        logit = sb("logit", [128, 8, TILES])
        whl = sb("whl", [128, TILES, 16])
        ident = const[:, C_ID:C_ID + 128]

        work = sb("work", [128, 5120])
        ring = sb("ring", [128, 3072], F32R)
        P = [work[:, 1536 * k:1536 * k + 1536] for k in range(2)]
        sel_in = work[0:16, 0:ROUTED * 128]
        v_sb = work[:, 3072:4096].rearrange("p (s h c) -> p s h c", s=2, h=HEADS)
        q4 = [ring[:, 256 * k:256 * k + 256] for k in range(4)]
        q4b = [ring[:, 1024 + 256 * k:1280 + 256 * k] for k in range(2)]
        k4 = [ring[:, 1536 + 256 * k:1792 + 256 * k] for k in range(2)]
        xh = ring[:, 2048:2304]
        xl = ring[:, 2304:2560]
        kz = [sb(f"kz{k}", [128, 4, 256], F32R) for k in range(2)]
        mexp = [sb(f"mexp{k}", [128, 2, 128], F32R) for k in range(2)]
        negm = sb("negm", [128, 2, 4])
        hi4 = sb("hi4", [128, 512], F32R)
        ot = sb("ot", [128, 256])
        on = sb("on", [128, 2, 128])
        rden = sb("rden", [128, 2, 4])
        xn = sb("xn", [128, 2, 128])
        wqk_h = sb("wqk_h", [128, 2, QUADS, 128], F32R)
        wqk_l = sb("wqk_l", [128, 2, QUADS, 128], F32R)
        mask_b = sb("mask_b", [128, 128], BF16)
        ident_b = sb("ident_b", [128, 128], BF16)
        stats = sb("stats", [128, TILES, 6])
        mv = sb("mv", [128, TILES, 2])
        rstd = sb("rstd", [128, TILES])
        std = sb("std", [128, TILES])
        eps = sb("eps", [128, 1])
        stage = sb("stage", [128, PIECE])
        s_b = [work[:, 512 * k:512 * k + 512] for k in range(2)]
        hf = [work[:, 1024 + 512 * k:1536 + 512 * k] for k in range(2)]
        wb = [work[:, 2048 + 512 * k:2560 + 512 * k] for k in range(2)]
        acc = work[:, 3072:3584]
        yt = work[:, 3584:4096]
        ob = work[:, 4096:4608].rearrange("p (t e) -> p t e", t=TPC)
        hh = [ring[:, 1024 * k:1024 * k + 512] for k in range(3)]
        hl = [ring[:, 1024 * k + 512:1024 * k + 1024] for k in range(3)]
        oh, ol = [kz[0][:, 2 * k:2 * k + 2, :].rearrange("p a b -> p (a b)") for k in range(2)]
        wst = sb("wst", [128, TPC, 16])
        wtc = kz[1][0:16, 0:2, :].rearrange("p a b -> p (a b)")
        r_a, r_b, r_c, r_s = [work[:, 3072 + 256 * k:3328 + 256 * k].rearrange("p (e t) -> p e t", t=TILES)
                              for k in range(4)]

        ps = ctx.enter_context(nc.psum_tensor("ps", [128, 8, 512], F32))
        S0, J, X = ps[:, 0, :], ps[:, 6, :], ps[:, 7, :]
        S1 = ps[:, 1:3, :]
        T0 = ps[:, 3:5, :].rearrange("p b c -> p (b c)")
        T1 = ps[:, 5, :]
        G, U, Y = [ps[:, 0, :], ps[:, 1, :]], [ps[:, 2, :], ps[:, 3, :]], [ps[:, 4, :], ps[:, 5, :]]
        WB, FT = ps[:, 6, :], ps[:, 7, :]

        s_in = [sem(f"s_in{k}") for k in range(4)]
        s_cst = sem("s_cst")
        s_prep = sem("s_prep")
        s_std = sem("s_std")
        s_ms = sem("s_ms")
        names = ("proj hi q4 k4 S1 S0 maxa maxb mhi mx Mt q4b ST0 ST1 ea eb sel PV OT T rc nm "
                 "xn xT xh xl V va lg tT oT wcp wsp wld "
                 "var G U s mul hh hlP hlD dn B wbc yr acc0 add ohc olc wc wT wtc F ob out rt rx turnP turnS")
        s = {n: sem("s_" + n) for n in names.split()}
        s_kz = [sem(f"s_kz{k}") for k in range(2)]
        s_xp = sem("s_xp")

        w_v = w_d
        x_v = x_d.rearrange("b (s p) e -> p (b s) e", p=128)
        out_v = out_d.rearrange("b (s p) e -> p (b s) e", p=128)

        def steps(eng, body, groups, per, ahead, behind):
            total = groups * per
            last = groups - (1 if ahead else 0)

            def peeled(a, z):
                for n in range(a, z):
                    body(n // per, n % per, lambda off, n=n: 0 <= n + off < total)

            peeled(-ahead, per)
            with eng.Fori(1, last) as g:
                for k in range(per):
                    body(g, k, lambda off: True)
            peeled(last * per, total + behind)

        def pass_a(eng, body):
            steps(eng, body, NB, QUADS, 4, 2)

        def pass_b(eng, body):
            steps(eng, body, NC, TPX, 0, 6)

        def at(b, j, off):
            bb, jj = b + (j + off) // 4, (j + off) % 4
            return bb, jj, bb * 4 + (jj + 1)

        def kz_done(b, j, off):
            bb, jj, _ = at(b, j, off)
            return bb * 128 + 64 * (jj // 2 + 1)

        def batches(b, j, ok):
            if isinstance(b, int):
                return 0 <= b - 1 < NB, 0 <= b < NB, 0 <= b + 1 < NB
            return True, True, True

        def tl(c, u, off):
            v = (u + off) % TPX
            return c + (u + off) // TPX, v // 3, v % 3, v

        def split_ready(eng, c, u, off):
            cc, e, i, _ = tl(c, u, off)
            if i == 0:
                eng.wait_ge(s["hlP"], cc * EXP + (e + 1))
            else:
                eng.wait_ge(s["hlD"], cc * (2 * EXP) + (2 * e + i))

        block = ctx.enter_context(nc.Block())

        @block.sync
        def _(sp):
            sp.dma_start(const[:, :], const_d[:, 0:C_SEL]).then_inc(s_cst, 16)
            sp.dma_start(sel_in, const_d[0:16, C_SEL:C_ALL]).then_inc(s_cst, 16)
            sp.dma_start(small[:, :], small_d).then_inc(s_cst, 16)
            sp.dma_start(rb[:, :], rb_d.partition_broadcast(128)).then_inc(s_cst, 16)
            for k in range(4):
                sp.dma_start(x_sb[:, 8 * k:8 * k + 8, :], x_v[:, 8 * k:8 * k + 8, :]).then_inc(s_in[k], 16)

            def body(b, j, ok):
                if ok(2):
                    _, j2, m = at(b, j, 2)
                    sp.wait_ge(s["k4"], m)
                    sp.sem_inc(s["turnS"], 1)
                    if ok(0):
                        sp.wait_ge(s["ST1"], at(b, j, 0)[2])
                    else:
                        sp.wait_ge(s_ms, 2)
                    for h in range(4):
                        sp.dma_start(kz[j2 % 2][32 * h:32 * h + 32, h, :].bitcast(F32),
                                     k4[j2 % 2][32 * h:32 * h + 32, :].bitcast(F32)).then_inc(s_kz[j2 % 2], 16)
                _, _, nxt = batches(b, j, ok)
                if j == 2 and nxt:
                    sp.wait_ge(s["xh"], b + 2)
                    sp.wait_ge(s["xl"], b + 2)
                    sp.dma_start(xh_all[:, bass.ds((b + 1) * 256, 256)].bitcast(F32), xh.bitcast(F32)).then_inc(s_xp, 16)
                    sp.dma_start(xl_all[:, bass.ds((b + 1) * 256, 256)].bitcast(F32), xl.bitcast(F32)).then_inc(s_xp, 16)
                if j == 0 and batches(b, j, ok)[1]:
                    if not isinstance(b, int) or b > 0:
                        sp.wait_ge(s["wsp"], b)
                    sp.dma_start(stage[:, :], w_v[:, bass.ds(b * PIECE, PIECE)]).then_inc(s["wld"], 16)

            pass_a(sp, body)

            sp.sem_inc(s["out"], 16)

            def out_chunk(c):
                sp.wait_ge(s["ob"], c + 2)
                sp.dma_start(out_v[:, bass.ds(c * TPC, TPC), :], ob).then_inc(s["out"], 16)
                sp.wait_ge(s["out"], c * 16 + 32)
                sp.sem_inc(s["turnS"], 1)

            with sp.Fori(0, NC) as c:
                out_chunk(c)

        @block.gpsimd
        def _(pool):
            pool.memset(kz[0][:, :, :].bitcast(F32), 0.0).then_inc(s_ms, 1)
            pool.memset(kz[1][:, :, :].bitcast(F32), 0.0).then_inc(s_ms, 1)
            pool.memset(mexp[0][:, :, :].bitcast(F32), 0.0).then_inc(s_ms, 1)
            pool.memset(mexp[1][:, :, :].bitcast(F32), 0.0).then_inc(s_ms, 1)
            pool.memset(v_sb[:, :, :, :], 0.0).then_inc(s_ms, 1)
            pool.wait_ge(s_ms, 5)
            pool.memset(v_sb[:, :, :, HD:HD + 1], 1.0).then_inc(s_ms, 1)
            pool.memset(whl[:, :, :], 0.0).then_inc(s_ms, 1)

            def body(b, j, ok):
                if ok(0):
                    _, j0, m = at(b, j, 0)
                    for ev, o in (("ea", P[j0 % 2][:, 0:1024].rearrange("p (h q) -> p h q", h=4)[:, :, 0:128]),
                                  ("eb", P[j0 % 2][:, 1024:1536].rearrange("p (h q) -> p h q", h=4))):
                        pool.wait_ge(s[ev], m)
                        pool.sem_inc(s["turnP"], 1)
                        pool.affine_select(out=o, in_=o, compare_op=ALU.is_ge, fill=0.0, base=0,
                                           pattern=[[0, 4], [1, 128]], channel_multiplier=-1)\
                            .then_inc(s["sel"], 1)
                if j == 2 and batches(b, j, ok)[1]:
                    pool.wait_ge(s["wld"], b * 16 + 16)
                    cols = bass.ds(b * PIECE, PIECE)
                    pool.tensor_copy(wh_all[:, cols], stage[:, :]).then_inc(s["wcp"], 1)
                    pool.wait_ge(s["wcp"], b + 1)
                    pool.tensor_tensor(wl_all[:, cols], stage[:, :], wh_all[:, cols].bitcast(F32),
                                       ALU.subtract).then_inc(s["wsp"], 1)

            pass_a(pool, body)

            def tile(c, u, ok):
                t = c * TPX + u
                if ok(-1) and tl(c, u, -1)[2] == 0:
                    _, _, i, v = tl(c, u, -1)
                    r = ROWS[i]
                    pool.wait_ge(s["hh"], t)
                    pool.tensor_tensor(hl[v % 3][0:r, :], hf[v % 2][0:r, :], hh[v % 3][0:r, :].bitcast(F32),
                                       ALU.subtract).then_inc(s["hlP"], 1)
                if ok(-3) and u % 3 == 2:
                    cc, e, _, _ = tl(c, u, -3)
                    if e >= 1:
                        pool.wait_ge(s["yr"], cc * EXP + (e + 1))
                        pool.tensor_tensor(acc, acc, yt, ALU.add).then_inc(s["add"], 1)

            pass_b(pool, tile)

        @block.scalar
        def _(act):
            act.wait_ge(s["var"], 2)
            act.activation(std[:, :], mv[:, :, 1], ACT.Sqrt, bias=eps[:, 0:1]).then_inc(s_std, 1)

            def body(b, j, ok):
                prev, cur, nxt = batches(b, j, ok)
                if j == 1 and prev:
                    act.wait_ge(s["tT"], b)
                    act.activation(o_all[:, bass.ds((b - 1) * 256, 256)], X[:, 256:512], ACT.Copy)\
                        .then_inc(s["oT"], 1)
                if j == 1 and nxt:
                    act.wait_ge(s["xT"], b + 2)
                    if not isinstance(b, int) or b >= 0:
                        act.wait_ge(s_xp, b * 32 + 32)
                    act.activation(xh, J[:, 0:256], ACT.Copy).then_inc(s["xh"], 1)
                if ok(0):
                    _, j0, m = at(b, j, 0)
                    act.wait_ge(s["ST0"], m)
                    if ok(-2):
                        act.wait_ge(s["PV"], at(b, j, -2)[2])
                    act.activation(P[j0 % 2][:, 0:1024], T0, ACT.Exp, scale=SCALE).then_inc(s["ea"], 1)
                    act.wait_ge(s["ST1"], m)
                    act.activation(P[j0 % 2][:, 1024:1536], T1, ACT.Exp, scale=SCALE).then_inc(s["eb"], 1)
                if ok(-1):
                    _, _, m = at(b, j, -1)
                    act.wait_ge(s["PV"], m)
                    if ok(-2):
                        act.wait_ge(s["T"], at(b, j, -2)[2])
                    act.activation(ot[:, :], X[:, 0:256], ACT.Copy).then_inc(s["OT"], 1)
                if j == 0 and cur:
                    act.wait_ge(s["lg"], b + 1)
                    if not isinstance(b, int) or b > 0:
                        act.wait_ge(s["PV"], at(b, j, -1)[2])
                    else:
                        act.wait_ge(s_ms, 6)
                    act.activation(v_sb[:, :, :, 0:HD],
                                   J[:, 0:256].rearrange("p (s h d) -> p s h d", s=2, h=HEADS), ACT.Copy)\
                        .then_inc(s["va"], 1)
                if ok(3):
                    _, _, m = at(b, j, 3)
                    act.wait_ge(s["proj"], m)
                    if ok(2) :
                        act.wait_ge(s["k4"], at(b, j, 2)[2])
                    act.activation(hi4[:, 0:256], J[:, 0:256], ACT.Copy).then_inc(s["hi"], 1)
                    act.activation(hi4[:, 256:512], J[:, 256:512], ACT.Identity,
                                   bias=const[:, C_COL + 2:C_COL + 3]).then_inc(s["hi"], 1)

            pass_a(act, body)
            act.wait_ge(s["rt"], 3)
            act.activation(r_a[:, 0:7, :], r_b[:, 0:7, :], ACT.Exp).then_inc(s["rx"], 1)

            def tile(c, u, ok):
                t = c * TPX + u
                e, i = u // 3, u % 3
                if ok(0) and u == 0:
                    if ok(-TPX):
                        act.wait_ge(s["dn"], (c - 1) * TPX + 1)
                    act.activation(oh, o_all[:, bass.ds(c * CH, CH)], ACT.Copy).then_inc(s["ohc"], 1)
                if ok(0):
                    r = ROWS[i]
                    act.wait_ge(s["G"], t + 1)
                    if ok(-2):
                        act.wait_ge(s["mul"], t - 1)
                    act.activation(s_b[u % 2][0:r, :], G[u % 2][0:r, :], ACT.Silu).then_inc(s["s"], 1)
                if ok(-1):
                    v = tl(c, u, -1)[3]
                    r = ROWS[v % 3]
                    act.wait_ge(s["mul"], t)
                    if ok(-4):
                        act.wait_ge(s["dn"], t - 3)
                    act.activation(hh[v % 3][0:r, :], hf[v % 2][0:r, :], ACT.Copy).then_inc(s["hh"], 1)
                if ok(0) and u == 2:
                    act.wait_ge(s["wT"], c + 1)
                    act.activation(wtc, FT[0:16, :], ACT.Copy).then_inc(s["wtc"], 1)
                if ok(0) and e >= 1 and i == 1:
                    act.wait_ge(s["B"], c * ROUTED + e)
                    if e > 1 or ok(-TPX):
                        act.wait_ge(s["yr"], c * EXP + (e - 1))
                    act.activation(wb[e % 2], WB, ACT.Copy).then_inc(s["wbc"], 1)

            pass_b(act, tile)

        @block.tensor
        def _(pe):
            def mm3(out, wh, wl, xh_, xl_, start, stop):
                pe.matmul(out, wh, xh_, start=start, stop=False, skip_group_check=True)
                pe.matmul(out, wh, xl_, start=False, stop=False, skip_group_check=True)
                return pe.matmul(out, wl, xh_, start=False, stop=stop, skip_group_check=True)

            pe.wait_ge(s_prep, N_PREP)
            pe.wait_ge(s_ms, 4)

            def body(b, j, ok):
                prev, cur, nxt = batches(b, j, ok)
                if j == 1 and prev:
                    pe.wait_ge(s["nm"], b * 4)
                    for t in range(2):
                        last = pe.transpose(X[:, 256 + 128 * t:384 + 128 * t], on[:, t, :], ident)
                    last.then_inc(s["tT"], 1)
                if ok(1):
                    _, j1, m = at(b, j, 1)
                    pe.wait_ge(s["q4"], m)
                    pe.wait_ge(s_kz[j1 % 2], kz_done(b, j, 1))
                    if ok(0):
                        pe.wait_ge(s["q4b"], at(b, j, 0)[2])
                    for g in range(2):
                        pe.matmul(S1[:, g, :], q4[j1][:, 128:256],
                                  kz[j1 % 2][:, 2 * g:2 * g + 2, :].rearrange("p h k -> p (h k)"),
                                  start=True, stop=False, skip_group_check=True)
                        for h in range(2):
                            last = pe.matmul(S1[:, g, 256 * h + 128:256 * h + 256], ident_b[:, :], mask_b[:, :],
                                             start=False, stop=(h == 1), skip_group_check=True)
                    last.then_inc(s["S1"], 1)
                    pe.matmul(S0, q4[j1][:, 0:128], kz[j1 % 2][:, :, 0:128], start=True, stop=False,
                              skip_group_check=True)
                    for h in range(4):
                        last = pe.matmul(S0[:, 128 * h:128 * h + 128], ident_b[:, :], mask_b[:, :],
                                         start=False, stop=(h == 3), skip_group_check=True)
                    last.then_inc(s["S0"], 1)
                if j == 1 and nxt:
                    pe.wait_ge(s["xn"], b + 2)
                    for t in range(2):
                        last = pe.transpose(J[:, 128 * t:128 * t + 128], xn[:, t, :], ident)
                    last.then_inc(s["xT"], 1)
                if j == 0 and cur:
                    for t in range(2):
                        for k, (lh, w) in enumerate(((xh, small_h), (xl, small_h), (xh, small_l))):
                            pe.matmul(J[:, 128 * t:128 * t + 128], lh[:, 128 * t:128 * t + 128],
                                      w[:, S_IN + 256:S_IN + 384], start=(t == 0 and k == 0), stop=(k == 2),
                                      skip_group_check=True)
                            last = pe.matmul(J[:, 256 + 8 * t:264 + 8 * t], lh[:, 128 * t:128 * t + 128],
                                             w[:, S_R:S_R + 8], start=False, stop=(k == 2),
                                             skip_group_check=True)
                    last.then_inc(s["V"], 1)
                if ok(0):
                    _, j0, m = at(b, j, 0)
                    z = kz[j0 % 2]
                    if not ok(1):
                        pe.wait_ge(s["q4b"], m)
                    if ok(-1):
                        pe.wait_ge(s["ea"], at(b, j, -1)[2])
                    for h in range(4):
                        last = pe.matmul(T0[:, 256 * h:256 * h + 256], z[:, h, 0:128], q4b[j0 % 2],
                                         start=True, stop=True)
                    last.then_inc(s["ST0"], 1)
                    if ok(-1):
                        pe.wait_ge(s["eb"], at(b, j, -1)[2])
                    for h in range(4):
                        last = pe.matmul(T1[:, 128 * h:128 * h + 128], z[:, h, 128:256],
                                         q4b[j0 % 2][:, 128:256], start=True, stop=True)
                    last.then_inc(s["ST1"], 1)
                if ok(-1):
                    bb, j9, m = at(b, j, -1)
                    pe.wait_ge(s["sel"], m * 2)
                    pe.wait_ge(s["va"], bb + 1)
                    if ok(-2):
                        pe.wait_ge(s["nm"], at(b, j, -2)[2])
                    if j == 1 and prev:
                        pe.wait_ge(s["oT"], b)
                    for h in range(4):
                        pe.matmul(X[32 * h:32 * h + 32, 0:256], v_sb[:, 0, 4 * j9 + h, :],
                                  P[j9 % 2][:, 256 * h:256 * h + 256], start=True, stop=False,
                                  skip_group_check=True)
                    for h in range(4):
                        last = pe.matmul(X[32 * h:32 * h + 32, 128:256], v_sb[:, 1, 4 * j9 + h, :],
                                         P[j9 % 2][:, 1024 + 128 * h:1152 + 128 * h], start=False, stop=True,
                                         skip_group_check=True)
                    last.then_inc(s["PV"], 1)
                if ok(3):
                    bb, j3, m = at(b, j, 3)
                    pe.wait_ge(s["xh"], bb + 1)
                    pe.wait_ge(s["xl"], bb + 1)
                    if j == 0 and cur:
                        pe.wait_ge(s["va"], b + 1)
                        pe.wait_ge(s["lg"], b + 1)
                    if ok(2):
                        pe.wait_ge(s["k4"], at(b, j, 2)[2])
                    for w in range(2):
                        last = mm3(J[:, 256 * w:256 * w + 256], wqk_h[:, w, j3, :], wqk_l[:, w, j3, :],
                                   xh, xl, w == 0, w == 1)
                    last.then_inc(s["proj"], 1)
                if ok(-1):
                    _, _, m = at(b, j, -1)
                    pe.wait_ge(s["OT"], m)
                    for t in range(2):
                        last = pe.transpose(X[:, 256 + 128 * t:384 + 128 * t], ot[:, 128 * t:128 * t + 128], ident)
                    last.then_inc(s["T"], 1)
                if ok(1):
                    _, j1, m = at(b, j, 1)
                    pe.wait_ge(s["mx"], m)
                    for t in range(2):
                        last = pe.matmul(S0[:, 128 * t:128 * t + 128], mexp[j1 % 2][:, t, :], ident_r[:, :],
                                         start=True, stop=True)
                    last.then_inc(s["Mt"], 1)

            pass_a(pe, body)
            pe.wait_ge(s["oT"], NB)
            pe.wait_ge(s_xp, NB * 32)
            pe.wait_ge(s["wsp"], NB)

            def tile(c, u, ok):
                e, i = u // 3, u % 3
                t = c * TPX + u
                if ok(0) and u == 1:
                    pe.wait_ge(s["wc"], c + 1)
                    if ok(-TPX):
                        pe.wait_ge(s["ob"], c)
                    for k in range(TPC):
                        last = pe.transpose(FT[0:16, 128 * k:128 * k + 128], wst[:, k, :], ident)
                    last.then_inc(s["wT"], 1)
                if ok(0) and e >= 1 and i == 0:
                    if e == 1:
                        pe.wait_ge(s["wtc"], c + 1)
                    if e > 1 or ok(-TPX):
                        pe.wait_ge(s["wbc"], c * ROUTED + (e - 1))
                    pe.matmul(WB, sel_r[:, 128 * (e - 1):128 * e], wtc, start=True, stop=True)\
                        .then_inc(s["B"], 1)
                if ok(0):
                    r = ROWS[i]
                    if ok(-2):
                        pe.wait_ge(s["mul"], t - 1)
                    xs = [a[:, bass.ds(c * CH, CH)] for a in (xh_all, xl_all)]
                    for k, (o, ev) in enumerate(((G[u % 2], "G"), (U[u % 2], "U"))):
                        w0 = e * WE + k * INNER + 128 * i
                        mm3(o[0:r, :], wh_all[:, w0:w0 + r], wl_all[:, w0:w0 + r], *xs, True, True)\
                            .then_inc(s[ev], 1)
                if ok(-2):
                    cc, de, di, v = tl(c, u, -2)
                    r = ROWS[di]
                    if di == 0 and ok(-8):
                        pe.wait_ge(s["yr"], cc * EXP + (de - 1))
                    if v == 0:
                        pe.wait_ge(s["ohc"], cc + 1)
                        pe.wait_ge(s["olc"], cc + 1)
                        mm3(Y[0], small_h[:, S_OUT:S_OUT + 128], small_l[:, S_OUT:S_OUT + 128],
                            oh, ol, True, False)
                    pe.wait_ge(s["hh"], t - 1)
                    split_ready(pe, c, u, -2)
                    w0 = de * WE + 2 * INNER + 128 * di
                    mm3(Y[de % 2], wh_all[0:r, w0:w0 + 128], wl_all[0:r, w0:w0 + 128],
                        hh[v % 3][0:r, :], hl[v % 3][0:r, :], di == 0 and v > 0, di == 2)\
                        .then_inc(s["dn"], 1)
                if u == 4 and ok(-TPX):
                    pe.wait_ge(s["add"], c * ROUTED)
                    if ok(0):
                        pe.wait_ge(s["wtc"], c + 1)
                    for k in range(TPC):
                        last = pe.transpose(FT[:, 128 * k:128 * k + 128], acc[:, 128 * k:128 * k + 128], ident)
                    last.then_inc(s["F"], 1)

            pass_b(pe, tile)

        @block.vector
        def _(dve):
            chain = [0]

            def link(ins, wait=True):
                chain[0] += 1
                ins.then_inc(s_prep, 1)
                if wait:
                    dve.wait_ge(s_prep, chain[0])

            dve.memset(eps[:, :], EPS)
            for k in range(4):
                dve.wait_ge(s_in[k], 16)
                for t in range(8 * k, 8 * k + 8):
                    last = dve.bn_stats(stats[:, t, :], x_sb[:, t, :])
            last.then_inc(s["var"], 1)
            dve.wait_ge(s["var"], 1)
            for t in range(TILES):
                last = dve.bn_aggr(mv[:, t, :], stats[:, t, :])
            last.then_inc(s["var"], 1)
            dve.wait_ge(s_cst, 64)
            dve.tensor_copy(ident_r[:, :], ident)
            dve.tensor_copy(ident_b[:, :], ident)
            dve.tensor_copy(mask_b[:, :], const[:, C_MASK:C_MASK + 128])
            dve.tensor_copy(sel_r[:, :], sel_in)
            link(dve.tensor_copy(small_h[:, :], small[:, :]))
            link(dve.tensor_tensor(small_l[:, :], small[:, :], small_h[:, :].bitcast(F32), ALU.subtract))
            for src, dst in ((small_h, wqk_h), (small_l, wqk_l)):
                link(dve.memset(dst[:, :, :, :].bitcast(F32), 0.0))
                for w in range(2):
                    v = src[:, S_IN + 128 * w:S_IN + 128 * w + 128].bitcast(F32)
                    v = v.rearrange("p (h d) -> p h d", h=HEADS)
                    o = dst[:, w, :, :].rearrange("p q (h c) -> p (q h) c", h=4)
                    for r in range(3):
                        link(dve.tensor_copy(o[:, :, HD * r:HD * r + HD], v), wait=False)
            dve.wait_ge(s_std, 1)
            link(dve.reciprocal(rstd[:, :], std[:, :]))
            assert chain[0] == N_PREP

            def body(b, j, ok):
                prev, cur, nxt = batches(b, j, ok)
                if j == 0 and nxt:
                    if ok(-4) or cur:
                        dve.wait_ge(s["xT"], b + 1)
                    for t in range(2):
                        k = (b + 1) * 2 + t
                        last = dve.tensor_scalar(xn[:, t, :], x_sb[:, bass.ds(k, 1), :].rearrange("p a e -> p (a e)"),
                                                 mv[:, bass.ds(k, 1), 0], rstd[:, bass.ds(k, 1)],
                                                 ALU.subtract, ALU.mult)
                    last.then_inc(s["xn"], 1)
                if ok(1):
                    _, j1, m = at(b, j, 1)
                    dve.wait_ge(s["S1"], m)
                    if ok(0):
                        dve.wait_ge(s["mx"], at(b, j, 0)[2])
                    dve.tensor_reduce(negm[:, 1, :], S1.rearrange("p g (h k) -> p (g h) k", h=2), AX.X,
                                      ALU.max, negate=True).then_inc(s["maxa"], 1)
                if j == 1 and nxt:
                    dve.wait_ge(s["xh"], b + 2)
                    if cur:
                        dve.wait_ge(s_xp, b * 32 + 32)
                    dve.tensor_tensor(xl, J[:, 0:256], xh.bitcast(F32), ALU.subtract).then_inc(s["xl"], 1)
                if ok(1):
                    dve.wait_ge(s["S0"], m)
                    dve.tensor_reduce(negm[:, 0, :], S0.rearrange("p (h k) -> p h k", h=4), AX.X,
                                      ALU.max, negate=True).then_inc(s["maxb"], 1)
                    slots = mexp[j1 % 2].rearrange("p t (h c) -> p t h c", c=32)
                    dve.wait_ge(s["maxa"], m)
                    dve.wait_ge(s["maxb"], m)
                    if ok(-1):
                        dve.wait_ge(s["Mt"], at(b, j, -1)[2])
                    else:
                        dve.wait_ge(s_ms, 4)
                    dve.tensor_copy(slots[:, :, :, 24], negm[:, :, :]).then_inc(s["mhi"], 1)
                    dve.wait_ge(s["mhi"], m)
                    dve.tensor_tensor(slots[:, :, :, 25], negm[:, :, :], slots[:, :, :, 24].bitcast(F32),
                                      ALU.subtract).then_inc(s["mx"], 1)
                if j == 0 and cur:
                    dve.wait_ge(s["V"], b + 1)
                    dve.tensor_copy(logit[:, :, bass.ds(b * 2, 2)],
                                    J[:, 256:272].rearrange("p (t e) -> p e t", t=2)).then_inc(s["lg"], 1)
                if ok(3):
                    _, j3, m3 = at(b, j, 3)
                    dve.wait_ge(s["hi"], m3 * 2)
                    if ok(-1):
                        dve.wait_ge(s["q4b"], at(b, j, -1)[2])
                    dve.scalar_tensor_tensor(q4[j3], hi4[:, 0:256].bitcast(F32), const[:, C_COL:C_COL + 1],
                                             J[:, 0:256], ALU.mult, ALU.add).then_inc(s["q4"], 1)
                    if ok(1):
                        dve.wait_ge(s_kz[(j + 1) % 2], kz_done(b, j, 1))
                    dve.scalar_tensor_tensor(k4[j3 % 2], hi4[:, 256:512].bitcast(F32),
                                             const[:, C_COL + 1:C_COL + 2], J[:, 256:512], ALU.mult, ALU.add)\
                        .then_inc(s["k4"], 1)
                if ok(-1):
                    _, j9, m9 = at(b, j, -1)
                    view = X[:, 256:512].rearrange("p (t h c) -> p t h c", t=2, c=32)
                    dve.wait_ge(s["T"], m9)
                    if ok(-2):
                        dve.wait_ge(s["nm"], at(b, j, -2)[2])
                    dve.reciprocal(rden[:, :, :], view[:, :, :, HD]).then_inc(s["rc"], 1)
                    dve.wait_ge(s["rc"], m9)
                    if j == 1 and prev:
                        dve.wait_ge(s["tT"], b)
                    dve.tensor_tensor(on[:, :, 32 * j9:32 * j9 + 32].rearrange("p t (h d) -> p t h d", h=4),
                                      view[:, :, :, 0:HD], rden[:, :, :].unsqueeze(3).to_broadcast([128, 2, 4, HD]),
                                      ALU.mult).then_inc(s["nm"], 1)
                if ok(1):
                    dve.wait_ge(s["Mt"], m)
                    if ok(-1):
                        dve.wait_ge(s["ST1"], at(b, j, -1)[2])
                    dve.tensor_tensor(q4b[j1 % 2], S0[:, 0:256], q4[j1].bitcast(F32), ALU.add)\
                        .then_inc(s["q4b"], 1)

            pass_a(dve, body)

            cnt = [0]

            def rt(ins):
                cnt[0] += 1
                ins.then_inc(s["rt"], 1)
                dve.wait_ge(s["rt"], cnt[0])

            n = ROUTED

            def over(ap):
                return ap.unsqueeze(1).to_broadcast([128, n, TILES])

            dve.wait_ge(s["lg"], NB)
            rt(dve.tensor_tensor(r_a[:, 0:n, :], logit[:, 0:n, :],
                                 rb[:, 0:n].unsqueeze(2).to_broadcast([128, n, TILES]), ALU.add))
            rt(dve.tensor_reduce(r_s[:, 0, :], r_a[:, 0:n, :].rearrange("p e t -> p t e"), AX.X, ALU.max))
            rt(dve.tensor_tensor(r_b[:, 0:n, :], r_a[:, 0:n, :], over(r_s[:, 0, :]), ALU.subtract))
            dve.wait_ge(s["rx"], 1)
            rt(dve.tensor_reduce(r_s[:, 1, :], r_a[:, 0:n, :].rearrange("p e t -> p t e"), AX.X, ALU.add))
            rt(dve.reciprocal(r_s[:, 2, :], r_s[:, 1, :]))
            rt(dve.tensor_tensor(r_a[:, 0:n, :], r_a[:, 0:n, :], over(r_s[:, 2, :]), ALU.mult))
            for e in range(n):
                rt(dve.memset(r_b[:, e, :], float(n - 1 - e)))
            for d in range(1, n):
                rt(dve.tensor_tensor(r_c[:, 0:n - d, :], r_a[:, 0:n - d, :], r_a[:, d:n, :], ALU.is_ge))
                rt(dve.tensor_tensor(r_b[:, d:n, :], r_b[:, d:n, :], r_c[:, 0:n - d, :], ALU.add))
                rt(dve.tensor_tensor(r_b[:, 0:n - d, :], r_b[:, 0:n - d, :], r_c[:, 0:n - d, :], ALU.subtract))
            rt(dve.tensor_scalar(r_c[:, 0:n, :], r_b[:, 0:n, :], 1.5, None, ALU.is_lt))
            rt(dve.tensor_tensor(r_c[:, 0:n, :], r_c[:, 0:n, :], r_a[:, 0:n, :], ALU.mult))
            rt(dve.tensor_reduce(r_s[:, 0, :], r_c[:, 0:n, :].rearrange("p e t -> p t e"), AX.X, ALU.add))
            rt(dve.reciprocal(r_s[:, 1, :], r_s[:, 0, :]))
            rt(dve.tensor_tensor(r_b[:, 0:n, :], r_c[:, 0:n, :], over(r_s[:, 1, :]), ALU.mult))
            dve.wait_ge(s_ms, 7)
            w_te = r_b[:, 0:n, :].rearrange("p e t -> p t e")
            rt(dve.tensor_copy(whl[:, :, 0:n].bitcast(F32R), w_te))
            rt(dve.tensor_tensor(whl[:, :, 8:8 + n], w_te, whl[:, :, 0:n], ALU.subtract))

            dve.sem_inc(s["ob"], 1)

            def tile(c, u, ok):
                t = c * TPX + u
                e, i = u // 3, u % 3
                if ok(0) and u == 0:
                    if ok(-TPX):
                        dve.wait_ge(s["wT"], c)
                    dve.tensor_copy(wst[:, :, :], whl[:, bass.ds(c * TPC, TPC), :]).then_inc(s["wc"], 1)
                    dve.wait_ge(s["ohc"], c + 1)
                    dve.tensor_tensor(ol, o_all[:, bass.ds(c * CH, CH)], oh.bitcast(F32),
                                      ALU.subtract).then_inc(s["olc"], 1)
                if ok(0):
                    r = ROWS[i]
                    dve.wait_ge(s["s"], t + 1)
                    dve.wait_ge(s["U"], t + 1)
                    if ok(-2):
                        dve.wait_ge(s["hh"], t - 1)
                        split_ready(dve, c, u, -2)
                    dve.tensor_tensor(hf[u % 2][0:r, :], U[u % 2][0:r, :], s_b[u % 2][0:r, :], ALU.mult)\
                        .then_inc(s["mul"], 1)
                if ok(-1) and tl(c, u, -1)[2] != 0:
                    v = tl(c, u, -1)[3]
                    r = ROWS[v % 3]
                    dve.wait_ge(s["hh"], t)
                    dve.tensor_tensor(hl[v % 3][0:r, :], hf[v % 2][0:r, :], hh[v % 3][0:r, :].bitcast(F32),
                                      ALU.subtract).then_inc(s["hlD"], 1)
                if u == 5 and ok(-TPX):
                    dve.wait_ge(s["F"], c)
                    dve.wait_ge(s["out"], c * 16)
                    dve.tensor_tensor(ob, FT.rearrange("p (t e) -> p t e", t=TPC),
                                      x_sb[:, bass.ds((c - 1) * TPC, TPC), :], ALU.add).then_inc(s["ob"], 1)
                if ok(-3) and i == 2:
                    cc, ye, _, _ = tl(c, u, -3)
                    dve.wait_ge(s["dn"], t - 2)
                    if ye == 0:
                        if ok(-TPX):
                            dve.wait_ge(s["F"], cc)
                        dve.tensor_copy(acc, Y[0]).then_inc(s["yr"], 1)
                    else:
                        dve.wait_ge(s["wbc"], cc * ROUTED + ye)
                        if ok(-6) and ye > 1 or ok(-TPX):
                            dve.wait_ge(s["add"], cc * ROUTED + (ye - 1))
                        dve.tensor_tensor(yt, Y[ye % 2], wb[ye % 2], ALU.mult).then_inc(s["yr"], 1)

            pass_b(dve, tile)


def kernel(**inputs):
    import concourse.bacc as bacc
    from concourse.bass_utils import run_bass_kernel_spmd

    f = {k.split("_", 1)[1]: np.asarray(v) for k, v in inputs.items()}
    gate = np.concatenate([f["ffn_sg"][None], f["ffn_rg"]])
    up = np.concatenate([f["ffn_su"][None], f["ffn_ru"]])
    down = np.concatenate([f["ffn_sd"][None], f["ffn_rd"]])
    down = np.pad(down, ((0, 0), (0, 0), (0, 3 * 128 - INNER)))
    down = down.reshape(EXP, EMB, 3, 128).transpose(3, 0, 2, 1).reshape(128, EXP, 3 * EMB)
    w = np.concatenate([gate.transpose(2, 0, 1), up.transpose(2, 0, 1), down], axis=2)
    small = np.concatenate([f["attn_in_proj_weight"].T, f["attn_out_proj_weight"].T,
                            np.pad(f["ffn_wr"], ((0, 1), (0, 0))).T], axis=1)
    arrays = {
        "x": np.ascontiguousarray(f["attn_query"]),
        "small": np.ascontiguousarray(small),
        "rb": np.pad(f["ffn_rb"], (0, 1)),
        "w": np.ascontiguousarray(w.reshape(128, EXP * WE)),
        "consts": constants(),
    }
    nc = bacc.Bacc("TRN2", target_bir_lowering=False, num_devices=1)
    aps = [nc.dram_tensor(k, a.shape, F32, kind="ExternalInput").ap() for k, a in arrays.items()]
    out = nc.dram_tensor("out", (NB, SEQ, EMB), F32, kind="ExternalOutput").ap()
    build(nc, *aps, out)
    return run_bass_kernel_spmd(nc, [arrays], core_ids=[0]).results[0]["out"]
```

```python
from contextlib import ExitStack

import numpy as np

import concourse.bass as bass
from concourse import mybir

F32 = mybir.dt.float32
F32R = mybir.dt.float32r
BF16 = mybir.dt.bfloat16
ALU = mybir.AluOpType
ACT = mybir.ActivationFunctionType
AX = mybir.AxisListType

NB, SEQ, EMB = 16, 256, 128
HEADS, HD = 16, 8
QUADS = 4
NQ = NB * QUADS
TILES = NB * SEQ // 128
TPC = 4
CH = TPC * 128
NC = TILES // TPC
EXP, INNER = 8, 352
ROUTED = EXP - 1
TPX = EXP * 3
ROWS = [128, 128, INNER - 256]
WE = 2 * INNER + 3 * 128
PIECE = EXP * WE // NB
N_MS = 9
N_PREP = 17
NEG = -1e30
SCALE = float(HD) ** -0.5
EPS = 1e-5
C_ID, C_MASK, C_COL, C_SEL = 0, 128, 256, 260
C_ALL = C_SEL + ROUTED
S_IN, S_OUT, S_R, S_ALL = 0, 384, 512, 520


def constants():
    c = np.zeros((128, C_ALL), np.float32)
    p = np.arange(128)
    c[:, C_ID:C_ID + 128] = np.eye(128)
    c[:, C_MASK:C_MASK + 128] = np.where(p[:, None] >= p[None, :], 0.0, NEG)
    part = p % 32 // HD
    c[:, C_COL] = part == 1
    c[:, C_COL + 1] = part == 2
    c[(p % 32 == 24) | (p % 32 == 25), C_COL + 2] = -1.0
    for r in range(ROUTED):
        c[r, C_SEL + r] = 1.0
        c[8 + r, C_SEL + r] = 1.0
    return c


def build(nc, x_d, small_d, rb_d, w_d, const_d, out_d):
    with ExitStack() as ctx:
        def sb(name, shape, dt=F32):
            return ctx.enter_context(nc.sbuf_tensor("sb_" + name, shape, dt))

        def sem(name):
            return ctx.enter_context(nc.semaphore(name))

        x_sb = sb("x_sb", [128, TILES, 128])
        xh_all = sb("xh_all", [128, NB * SEQ], F32R)
        xl_all = sb("xl_all", [128, NB * SEQ], F32R)
        o_all = sb("o_all", [128, NB * SEQ])
        wh_all = sb("wh_all", [128, EXP * WE], F32R)
        wl_all = sb("wl_all", [128, EXP * WE], F32R)
        const = sb("const", [128, C_ALL])
        ident_r = sb("ident_r", [128, 128], F32R)
        small = sb("small", [128, S_ALL])
        small_h = sb("small_h", [128, S_ALL], F32R)
        small_l = sb("small_l", [128, S_ALL], F32R)
        rb = sb("rb", [128, 8])
        logit = sb("logit", [128, 8, TILES])
        whl = sb("whl", [128, TILES, 16])
        ident = const[:, C_ID:C_ID + 128]

        work = sb("work", [128, 4096])
        ring = sb("ring", [128, 3072], F32R)
        P = [work[:, 1536 * k:1536 * k + 1536] for k in range(2)]
        v_sb = work[:, 3072:4096].rearrange("p (s h c) -> p s h c", s=2, h=HEADS)
        qk4 = [ring[:, 512 * k:512 * k + 512] for k in range(4)]
        q4 = [qk4[k][:, 0:256] for k in range(4)]
        k4 = [qk4[k][:, 256:512] for k in range(4)]
        q4b = [ring[:, 2048 + 256 * k:2304 + 256 * k] for k in range(2)]
        xh = ring[:, 2560:2816]
        xl = ring[:, 2816:3072]
        kz = [sb(f"kz{k}", [128, 4, 256], F32R) for k in range(4)]
        mexp = [sb(f"mexp{k}", [128, 2, 128], F32R) for k in range(2)]
        negm = sb("negm", [128, 2, 4])
        hi4 = sb("hi4", [128, 512], F32R)
        ot = sb("ot", [128, 256])
        vt = sb("vt", [128, 256])[:, :]
        on = sb("on", [128, 2, 128])
        rden = sb("rden", [128, 2, 4])
        xn = sb("xn", [128, 2, 128])
        wqk_h = sb("wqk_h", [128, 2, QUADS, 128], F32R)
        wqk_l = sb("wqk_l", [128, 2, QUADS, 128], F32R)
        mask_b = sb("mask_b", [128, 128], BF16)
        ident_b = sb("ident_b", [128, 128], BF16)
        stats = sb("stats", [128, TILES, 6])
        mv = sb("mv", [128, TILES, 2])
        rstd = sb("rstd", [128, TILES])
        std = sb("std", [128, TILES])
        eps = sb("eps", [128, 1])
        stage = sb("stage", [128, PIECE])
        s_b = [work[:, 512 * k:512 * k + 512] for k in range(2)]
        hf = [work[:, 1024 + 512 * k:1536 + 512 * k] for k in range(2)]
        wb = [work[:, 2048 + 512 * k:2560 + 512 * k] for k in range(2)]
        acc = work[:, 3072:3584]
        yt = work[:, 3584:4096]
        sel_r = wqk_h[0:16, :, :, :].rearrange("p w q c -> p (w q) c")
        ob = stage[:, 0:CH].rearrange("p (t e) -> p t e", t=TPC)
        hh = [ring[:, 1024 * k:1024 * k + 512] for k in range(3)]
        hl = [ring[:, 1024 * k + 512:1024 * k + 1024] for k in range(3)]
        oh, ol = [kz[0][:, 2 * k:2 * k + 2, :].rearrange("p a b -> p (a b)") for k in range(2)]
        wst = sb("wst", [128, TPC, 16])
        wtc = kz[1][0:16, 0:2, :].rearrange("p a b -> p (a b)")
        r_a, r_b, r_c, r_s = [work[:, 3072 + 256 * k:3328 + 256 * k].rearrange("p (e t) -> p e t", t=TILES)
                              for k in range(4)]

        ps = ctx.enter_context(nc.psum_tensor("ps", [128, 8, 512], F32))
        S0, J, X = ps[:, 0, :], ps[:, 6, :], ps[:, 7, :]
        S1 = ps[:, 1:3, :]
        T0 = ps[:, 3:5, :].rearrange("p b c -> p (b c)")
        T1 = ps[:, 5, :]
        G, U, Y = [ps[:, 0, :], ps[:, 1, :]], [ps[:, 2, :], ps[:, 3, :]], [ps[:, 4, :], ps[:, 5, :]]
        WB, FT = ps[:, 6, :], ps[:, 7, :]

        s_in = [sem(f"s_in{k}") for k in range(4)]
        s_cst = sem("s_cst")
        s_prep = sem("s_prep")
        s_std = sem("s_std")
        s_ms = sem("s_ms")
        names = ("proj hi k4 S1 S0 maxa maxb mhi mx Mt q4b ST0 ST1 ea eb sel PV OT T rc nm "
                 "xn xT xh xl V va lg tT oT wcp wsp wld "
                 "var G U s mul hh hlP hlD dn B wbc yr acc0 add ohc olc wc wT wtc F ob out rt rx turnP turnS vt")
        s = {n: sem("s_" + n) for n in names.split()}
        s_kz = [sem(f"s_kz{k}") for k in range(4)]
        s_xp = sem("s_xp")

        w_v = w_d
        x_v = x_d.rearrange("b (s p) e -> p (b s) e", p=128)
        out_v = out_d.rearrange("b (s p) e -> p (b s) e", p=128)

        def steps(eng, body, groups, per, ahead, behind):
            total = groups * per
            last = groups - (1 if ahead else 0)

            def peeled(a, z):
                for n in range(a, z):
                    body(n // per, n % per, lambda off, n=n: 0 <= n + off < total)

            peeled(-ahead, per)
            with eng.Fori(1, last) as g:
                for k in range(per):
                    body(g, k, lambda off: True)
            peeled(last * per, total + behind)

        def pass_a(eng, body):
            steps(eng, body, NB, QUADS, 4, 2)

        def pass_b(eng, body):
            steps(eng, body, NC, TPX, 0, 6)

        def at(b, j, off):
            bb, jj = b + (j + off) // 4, (j + off) % 4
            return bb, jj, bb * 4 + (jj + 1)

        def wait_kz(eng, b, j, off):
            bb, jj, _ = at(b, j, off)
            eng.wait_ge(s_kz[jj], bb * 64 + 64)

        def batches(b, j, ok):
            if isinstance(b, int):
                return 0 <= b - 1 < NB, 0 <= b < NB, 0 <= b + 1 < NB
            return True, True, True

        def tl(c, u, off):
            v = (u + off) % TPX
            return c + (u + off) // TPX, v // 3, v % 3, v

        def split_ready(eng, c, u, off):
            cc, e, i, _ = tl(c, u, off)
            if i == 0:
                eng.wait_ge(s["hlP"], cc * EXP + (e + 1))
            else:
                eng.wait_ge(s["hlD"], cc * (2 * EXP) + (2 * e + i))

        block = ctx.enter_context(nc.Block())

        @block.sync
        def _(sp):
            sp.dma_start(const[:, :], const_d).then_inc(s_cst, 16)
            sp.dma_start(small[:, :], small_d).then_inc(s_cst, 16)
            sp.dma_start(rb[:, :], rb_d.partition_broadcast(128)).then_inc(s_cst, 16)
            for k in range(4):
                sp.dma_start(x_sb[:, 8 * k:8 * k + 8, :], x_v[:, 8 * k:8 * k + 8, :]).then_inc(s_in[k], 16)

            def body(b, j, ok):
                if ok(3):
                    _, j3, m = at(b, j, 3)
                    sp.wait_ge(s["k4"], m)
                    sp.sem_inc(s["turnS"], 1)
                    if ok(-1):
                        sp.wait_ge(s["ST1"], at(b, j, -1)[2])
                    else:
                        sp.wait_ge(s_ms, N_MS)
                    for h in range(4):
                        sp.dma_start(kz[j3][32 * h:32 * h + 32, h, :].bitcast(F32),
                                     k4[j3][32 * h:32 * h + 32, :].bitcast(F32)).then_inc(s_kz[j3], 16)
                _, _, nxt = batches(b, j, ok)
                if j == 1 and nxt:
                    sp.wait_ge(s["xh"], b + 2)
                    sp.wait_ge(s["xl"], b + 2)
                    sp.dma_start(xh_all[:, bass.ds((b + 1) * 256, 256)].bitcast(F32), xh.bitcast(F32)).then_inc(s_xp, 16)
                    sp.dma_start(xl_all[:, bass.ds((b + 1) * 256, 256)].bitcast(F32), xl.bitcast(F32)).then_inc(s_xp, 16)
                if j == 0 and batches(b, j, ok)[1]:
                    if not isinstance(b, int) or b > 0:
                        sp.wait_ge(s["wsp"], b)
                    sp.dma_start(stage[:, :], w_v[:, bass.ds(b * PIECE, PIECE)]).then_inc(s["wld"], 16)

            pass_a(sp, body)

            sp.sem_inc(s["out"], 16)

            def out_chunk(c):
                sp.wait_ge(s["ob"], c + 2)
                sp.dma_start(out_v[:, bass.ds(c * TPC, TPC), :], ob).then_inc(s["out"], 16)
                sp.wait_ge(s["out"], c * 16 + 32)
                sp.sem_inc(s["turnS"], 1)

            with sp.Fori(0, NC) as c:
                out_chunk(c)

        @block.gpsimd
        def _(pool):
            for buf in (*kz, *mexp):
                pool.memset(buf[:, :, :].bitcast(F32), 0.0).then_inc(s_ms, 1)
            pool.memset(v_sb[:, :, :, :], 0.0).then_inc(s_ms, 1)
            pool.wait_ge(s_ms, N_MS - 2)
            pool.memset(v_sb[:, :, :, HD:HD + 1], 1.0).then_inc(s_ms, 1)
            pool.memset(whl[:, :, :], 0.0).then_inc(s_ms, 1)

            def body(b, j, ok):
                if j == 0 and batches(b, j, ok)[1]:
                    pool.wait_ge(s["vt"], b + 1)
                    if ok(-1):
                        pool.wait_ge(s["PV"], at(b, j, -1)[2])
                    else:
                        pool.wait_ge(s_ms, N_MS)
                    pool.sem_inc(s["turnP"], 1)
                    pool.tensor_copy(v_sb[:, :, :, 0:HD], vt.rearrange("p (s h d) -> p s h d", s=2, h=HEADS))\
                        .then_inc(s["va"], 1)
                if ok(0):
                    _, j0, m = at(b, j, 0)
                    for ev, o in (("ea", P[j0 % 2][:, 0:1024].rearrange("p (h q) -> p h q", h=4)[:, :, 0:128]),
                                  ("eb", P[j0 % 2][:, 1024:1536].rearrange("p (h q) -> p h q", h=4))):
                        pool.wait_ge(s[ev], m)
                        pool.sem_inc(s["turnP"], 1)
                        pool.affine_select(out=o, in_=o, compare_op=ALU.is_ge, fill=0.0, base=0,
                                           pattern=[[0, 4], [1, 128]], channel_multiplier=-1)\
                            .then_inc(s["sel"], 1)
                if j == 2 and batches(b, j, ok)[1]:
                    pool.wait_ge(s["wld"], b * 16 + 16)
                    cols = bass.ds(b * PIECE, PIECE)
                    pool.tensor_copy(wh_all[:, cols], stage[:, :]).then_inc(s["wcp"], 1)
                    pool.wait_ge(s["wcp"], b + 1)
                    pool.tensor_tensor(wl_all[:, cols], stage[:, :], wh_all[:, cols].bitcast(F32),
                                       ALU.subtract).then_inc(s["wsp"], 1)

            pass_a(pool, body)

            def tile(c, u, ok):
                t = c * TPX + u
                if ok(-1) and tl(c, u, -1)[2] == 0:
                    _, _, i, v = tl(c, u, -1)
                    r = ROWS[i]
                    pool.wait_ge(s["hh"], t)
                    pool.tensor_tensor(hl[v % 3][0:r, :], hf[v % 2][0:r, :], hh[v % 3][0:r, :].bitcast(F32),
                                       ALU.subtract).then_inc(s["hlP"], 1)
                if ok(-3) and u % 3 == 2:
                    cc, e, _, _ = tl(c, u, -3)
                    if e >= 1:
                        pool.wait_ge(s["yr"], cc * EXP + (e + 1))
                        pool.tensor_tensor(acc, acc, yt, ALU.add).then_inc(s["add"], 1)

            pass_b(pool, tile)

        @block.scalar
        def _(act):
            act.wait_ge(s["var"], 2)
            act.activation(std[:, :], mv[:, :, 1], ACT.Sqrt, bias=eps[:, 0:1]).then_inc(s_std, 1)

            def body(b, j, ok):
                prev, cur, nxt = batches(b, j, ok)
                if j == 1 and prev:
                    act.wait_ge(s["tT"], b)
                    act.activation(o_all[:, bass.ds((b - 1) * 256, 256)], X[:, 256:512], ACT.Copy)\
                        .then_inc(s["oT"], 1)
                if j == 0 and cur:
                    act.wait_ge(s["V"], b + 1)
                    if ok(-1):
                        act.wait_ge(s["va"], b)
                    act.activation(vt, J[:, 0:256], ACT.Copy).then_inc(s["vt"], 1)
                    act.activation(logit[:, :, bass.ds(b * 2, 2)],
                                   J[:, 256:272].rearrange("p (t e) -> p e t", t=2), ACT.Copy).then_inc(s["lg"], 1)
                if j == 0 and nxt:
                    act.wait_ge(s["xT"], b + 2)
                    if not isinstance(b, int) or b >= 0:
                        act.wait_ge(s_xp, b * 32 + 32)
                    act.activation(xh, J[:, 0:256], ACT.Copy).then_inc(s["xh"], 1)
                if ok(0):
                    _, j0, m = at(b, j, 0)
                    act.wait_ge(s["ST0"], m)
                    if ok(-2):
                        act.wait_ge(s["PV"], at(b, j, -2)[2])
                    act.activation(P[j0 % 2][:, 0:1024], T0, ACT.Exp, scale=SCALE).then_inc(s["ea"], 1)
                    act.wait_ge(s["ST1"], m)
                    act.activation(P[j0 % 2][:, 1024:1536], T1, ACT.Exp, scale=SCALE).then_inc(s["eb"], 1)
                if ok(-1):
                    _, _, m = at(b, j, -1)
                    act.wait_ge(s["PV"], m)
                    if ok(-2):
                        act.wait_ge(s["T"], at(b, j, -2)[2])
                    act.activation(ot[:, :], X[:, 0:256], ACT.Copy).then_inc(s["OT"], 1)
                if ok(4):
                    _, _, m = at(b, j, 4)
                    act.wait_ge(s["proj"], m)
                    if ok(3):
                        act.wait_ge(s["k4"], at(b, j, 3)[2])
                    for w in range(2):
                        act.activation(hi4[:, 256 * w:256 * w + 256], J[:, 256 * w:256 * w + 256], ACT.Identity,
                                       scale=const[:, C_COL + w:C_COL + w + 1],
                                       bias=const[:, C_COL + 2:C_COL + 3] if w else 0.0).then_inc(s["hi"], 1)

            pass_a(act, body)
            act.wait_ge(s["rt"], 4)
            act.activation(r_a[:, 0:7, :], r_b[:, 0:7, :], ACT.Exp).then_inc(s["rx"], 1)

            def tile(c, u, ok):
                t = c * TPX + u
                e, i = u // 3, u % 3
                if ok(0) and u == 0:
                    if ok(-TPX):
                        act.wait_ge(s["dn"], (c - 1) * TPX + 1)
                    act.activation(oh, o_all[:, bass.ds(c * CH, CH)], ACT.Copy).then_inc(s["ohc"], 1)
                if ok(0):
                    r = ROWS[i]
                    act.wait_ge(s["G"], t + 1)
                    if ok(-2):
                        act.wait_ge(s["mul"], t - 1)
                    act.activation(s_b[u % 2][0:r, :], G[u % 2][0:r, :], ACT.Silu).then_inc(s["s"], 1)
                if ok(-1):
                    v = tl(c, u, -1)[3]
                    r = ROWS[v % 3]
                    act.wait_ge(s["mul"], t)
                    if ok(-4):
                        act.wait_ge(s["dn"], t - 3)
                    act.activation(hh[v % 3][0:r, :], hf[v % 2][0:r, :], ACT.Copy).then_inc(s["hh"], 1)
                if ok(0) and u == 2:
                    act.wait_ge(s["wT"], c + 1)
                    act.activation(wtc, FT[0:16, :], ACT.Copy).then_inc(s["wtc"], 1)
                if ok(0) and e >= 1 and i == 1:
                    act.wait_ge(s["B"], c * ROUTED + e)
                    if e > 1 or ok(-TPX):
                        act.wait_ge(s["yr"], c * EXP + (e - 1))
                    act.activation(wb[e % 2], WB, ACT.Copy).then_inc(s["wbc"], 1)

            pass_b(act, tile)

        @block.tensor
        def _(pe):
            def mm3(out, wh, wl, xh_, xl_, start, stop):
                pe.matmul(out, wh, xh_, start=start, stop=False, skip_group_check=True)
                pe.matmul(out, wh, xl_, start=False, stop=False, skip_group_check=True)
                return pe.matmul(out, wl, xh_, start=False, stop=stop, skip_group_check=True)

            pe.wait_ge(s_prep, N_PREP)
            pe.wait_ge(s_ms, N_MS)

            def body(b, j, ok):
                prev, cur, nxt = batches(b, j, ok)
                if ok(1):
                    _, j1, m = at(b, j, 1)
                    pe.wait_ge(s["k4"], m)
                    wait_kz(pe, b, j, 1)
                    if ok(0):
                        pe.wait_ge(s["maxa"], at(b, j, 0)[2])
                    for g in range(2):
                        pe.matmul(S1[:, g, :], q4[j1][:, 128:256],
                                  kz[j1][:, 2 * g:2 * g + 2, :].rearrange("p h k -> p (h k)"),
                                  start=True, stop=False, skip_group_check=True)
                        diag = S1[:, g, :].rearrange("p (h k) -> p h k", h=2)[:, :, 128:256]
                        last = pe.matmul(diag, ident_b[:, :], mask_b[:, :].unsqueeze(1).to_broadcast([128, 2, 128]),
                                         start=False, stop=True, skip_group_check=True)
                    last.then_inc(s["S1"], 1)
                    if ok(0):
                        pe.wait_ge(s["q4b"], at(b, j, 0)[2])
                    pe.matmul(S0, q4[j1][:, 0:128], kz[j1][:, :, 0:128], start=True, stop=False,
                              skip_group_check=True)
                    last = pe.matmul(S0, ident_b[:, :], mask_b[:, :].unsqueeze(1).to_broadcast([128, 4, 128]),
                                     start=False, stop=True, skip_group_check=True)
                    last.then_inc(s["S0"], 1)
                if j == 1 and prev:
                    pe.wait_ge(s["nm"], b * 4)
                    for t in range(2):
                        last = pe.transpose(X[:, 256 + 128 * t:384 + 128 * t], on[:, t, :], ident)
                    last.then_inc(s["tT"], 1)
                if j == 0 and cur:
                    if ok(3):
                        pe.wait_ge(s["k4"], at(b, j, 3)[2])
                    for t in range(2):
                        for k, (lh, w) in enumerate(((xh, small_h), (xl, small_h), (xh, small_l))):
                            pe.matmul(J[:, 128 * t:128 * t + 128], lh[:, 128 * t:128 * t + 128],
                                      w[:, S_IN + 256:S_IN + 384], start=(t == 0 and k == 0), stop=(k == 2),
                                      skip_group_check=True)
                            last = pe.matmul(J[:, 256 + 8 * t:264 + 8 * t], lh[:, 128 * t:128 * t + 128],
                                             w[:, S_R:S_R + 8], start=False, stop=(k == 2),
                                             skip_group_check=True)
                    last.then_inc(s["V"], 1)
                if ok(0):
                    _, j0, m = at(b, j, 0)
                    z = kz[j0]
                    if not ok(1):
                        pe.wait_ge(s["q4b"], m)
                    if ok(-1):
                        pe.wait_ge(s["ea"], at(b, j, -1)[2])
                    for h in range(4):
                        last = pe.matmul(T0[:, 256 * h:256 * h + 256], z[:, h, 0:128], q4b[j0 % 2],
                                         start=True, stop=True)
                    last.then_inc(s["ST0"], 1)
                    if ok(-1):
                        pe.wait_ge(s["eb"], at(b, j, -1)[2])
                    for h in range(4):
                        last = pe.matmul(T1[:, 128 * h:128 * h + 128], z[:, h, 128:256],
                                         q4b[j0 % 2][:, 128:256], start=True, stop=True)
                    last.then_inc(s["ST1"], 1)
                if j == 0 and nxt:
                    pe.wait_ge(s["xn"], b + 2)
                    if cur:
                        pe.wait_ge(s["lg"], b + 1)
                    for t in range(2):
                        last = pe.transpose(J[:, 128 * t:128 * t + 128], xn[:, t, :], ident)
                    last.then_inc(s["xT"], 1)
                if ok(-1):
                    bb, j9, m = at(b, j, -1)
                    pe.wait_ge(s["sel"], m * 2)
                    pe.wait_ge(s["va"], bb + 1)
                    if ok(-2):
                        pe.wait_ge(s["nm"], at(b, j, -2)[2])
                    if j == 1 and prev:
                        pe.wait_ge(s["oT"], b)
                    for h in range(4):
                        pe.matmul(X[32 * h:32 * h + 32, 0:256], v_sb[:, 0, 4 * j9 + h, :],
                                  P[j9 % 2][:, 256 * h:256 * h + 256], start=True, stop=False,
                                  skip_group_check=True)
                    for h in range(4):
                        last = pe.matmul(X[32 * h:32 * h + 32, 128:256], v_sb[:, 1, 4 * j9 + h, :],
                                         P[j9 % 2][:, 1024 + 128 * h:1152 + 128 * h], start=False, stop=True,
                                         skip_group_check=True)
                    last.then_inc(s["PV"], 1)
                if ok(4):
                    bb, j4, m = at(b, j, 4)
                    pe.wait_ge(s["xh"], bb + 1)
                    pe.wait_ge(s["xl"], bb + 1)
                    if ok(3):
                        pe.wait_ge(s["k4"], at(b, j, 3)[2])
                    for w in range(2):
                        last = mm3(J[:, 256 * w:256 * w + 256], wqk_h[:, w, j4, :], wqk_l[:, w, j4, :],
                                   xh, xl, w == 0, w == 1)
                    last.then_inc(s["proj"], 1)
                if ok(-1):
                    _, _, m = at(b, j, -1)
                    pe.wait_ge(s["OT"], m)
                    for t in range(2):
                        last = pe.transpose(X[:, 256 + 128 * t:384 + 128 * t], ot[:, 128 * t:128 * t + 128], ident)
                    last.then_inc(s["T"], 1)
                if ok(1):
                    _, j1, m = at(b, j, 1)
                    pe.wait_ge(s["mx"], m)
                    for t in range(2):
                        last = pe.matmul(S0[:, 128 * t:128 * t + 128], mexp[j1 % 2][:, t, :], ident_r[:, :],
                                         start=True, stop=True)
                    last.then_inc(s["Mt"], 1)

            pass_a(pe, body)
            pe.wait_ge(s["oT"], NB)
            pe.wait_ge(s_xp, NB * 32)
            pe.wait_ge(s["wsp"], NB)

            def tile(c, u, ok):
                e, i = u // 3, u % 3
                t = c * TPX + u
                if ok(0) and u == 1:
                    pe.wait_ge(s["wc"], c + 1)
                    if ok(-TPX):
                        pe.wait_ge(s["ob"], c)
                    for k in range(TPC):
                        last = pe.transpose(FT[0:16, 128 * k:128 * k + 128], wst[:, k, :], ident)
                    last.then_inc(s["wT"], 1)
                if ok(0) and e >= 1 and i == 0:
                    if e == 1:
                        pe.wait_ge(s["wtc"], c + 1)
                    if e > 1 or ok(-TPX):
                        pe.wait_ge(s["wbc"], c * ROUTED + (e - 1))
                    pe.matmul(WB, sel_r[:, e - 1, :], wtc, start=True, stop=True)\
                        .then_inc(s["B"], 1)
                if ok(0):
                    r = ROWS[i]
                    if ok(-2):
                        pe.wait_ge(s["mul"], t - 1)
                    xs = [a[:, bass.ds(c * CH, CH)] for a in (xh_all, xl_all)]
                    for k, (o, ev) in enumerate(((G[u % 2], "G"), (U[u % 2], "U"))):
                        w0 = e * WE + k * INNER + 128 * i
                        mm3(o[0:r, :], wh_all[:, w0:w0 + r], wl_all[:, w0:w0 + r], *xs, True, True)\
                            .then_inc(s[ev], 1)
                if ok(-2):
                    cc, de, di, v = tl(c, u, -2)
                    r = ROWS[di]
                    if di == 0 and ok(-8):
                        pe.wait_ge(s["yr"], cc * EXP + (de - 1))
                    if v == 0:
                        pe.wait_ge(s["ohc"], cc + 1)
                        pe.wait_ge(s["olc"], cc + 1)
                        mm3(Y[0], small_h[:, S_OUT:S_OUT + 128], small_l[:, S_OUT:S_OUT + 128],
                            oh, ol, True, False)
                    pe.wait_ge(s["hh"], t - 1)
                    split_ready(pe, c, u, -2)
                    w0 = de * WE + 2 * INNER + 128 * di
                    mm3(Y[de % 2], wh_all[0:r, w0:w0 + 128], wl_all[0:r, w0:w0 + 128],
                        hh[v % 3][0:r, :], hl[v % 3][0:r, :], di == 0 and v > 0, di == 2)\
                        .then_inc(s["dn"], 1)
                if u == 4 and ok(-TPX):
                    pe.wait_ge(s["add"], c * ROUTED)
                    if ok(0):
                        pe.wait_ge(s["wtc"], c + 1)
                    for k in range(TPC):
                        last = pe.transpose(FT[:, 128 * k:128 * k + 128], acc[:, 128 * k:128 * k + 128], ident)
                    last.then_inc(s["F"], 1)

            pass_b(pe, tile)

        @block.vector
        def _(dve):
            chain = [0]

            def link(ins, wait=True):
                chain[0] += 1
                ins.then_inc(s_prep, 1)
                if wait:
                    dve.wait_ge(s_prep, chain[0])

            dve.memset(eps[:, :], EPS)
            for k in range(4):
                dve.wait_ge(s_in[k], 16)
                for t in range(8 * k, 8 * k + 8):
                    last = dve.bn_stats(stats[:, t, :], x_sb[:, t, :])
            last.then_inc(s["var"], 1)
            dve.wait_ge(s["var"], 1)
            for t in range(TILES):
                last = dve.bn_aggr(mv[:, t, :], stats[:, t, :])
            last.then_inc(s["var"], 1)
            dve.wait_ge(s_cst, 48)
            dve.tensor_copy(ident_r[:, :], ident)
            dve.tensor_copy(ident_b[:, :], ident)
            dve.tensor_copy(mask_b[:, :], const[:, C_MASK:C_MASK + 128])
            link(dve.tensor_copy(small_h[:, :], small[:, :]))
            link(dve.tensor_tensor(small_l[:, :], small[:, :], small_h[:, :].bitcast(F32), ALU.subtract))
            for src, dst in ((small_h, wqk_h), (small_l, wqk_l)):
                link(dve.memset(dst[:, :, :, :].bitcast(F32), 0.0))
                for w in range(2):
                    v = src[:, S_IN + 128 * w:S_IN + 128 * w + 128].bitcast(F32)
                    v = v.rearrange("p (h d) -> p h d", h=HEADS)
                    o = dst[:, w, :, :].rearrange("p q (h c) -> p (q h) c", h=4)
                    for r in range(3):
                        link(dve.tensor_copy(o[:, :, HD * r:HD * r + HD], v), wait=False)
            dve.wait_ge(s_std, 1)
            link(dve.reciprocal(rstd[:, :], std[:, :]))
            assert chain[0] == N_PREP

            def body(b, j, ok):
                prev, cur, nxt = batches(b, j, ok)
                if j == 0 and nxt:
                    if cur:
                        dve.wait_ge(s["xT"], b + 1)
                    for t in range(2):
                        k = (b + 1) * 2 + t
                        last = dve.tensor_scalar(xn[:, t, :], x_sb[:, bass.ds(k, 1), :].rearrange("p a e -> p (a e)"),
                                                 mv[:, bass.ds(k, 1), 0], rstd[:, bass.ds(k, 1)],
                                                 ALU.subtract, ALU.mult)
                    last.then_inc(s["xn"], 1)
                if ok(1):
                    _, j1, m = at(b, j, 1)
                    dve.wait_ge(s["S1"], m)
                    if ok(0):
                        dve.wait_ge(s["mx"], at(b, j, 0)[2])
                    dve.tensor_reduce(negm[:, 1, :], S1.rearrange("p g (h k) -> p (g h) k", h=2), AX.X,
                                      ALU.max, negate=True).then_inc(s["maxa"], 1)
                if ok(1):
                    dve.wait_ge(s["S0"], m)
                    dve.tensor_reduce(negm[:, 0, :], S0.rearrange("p (h k) -> p h k", h=4), AX.X,
                                      ALU.max, negate=True).then_inc(s["maxb"], 1)
                    slots = mexp[j1 % 2].rearrange("p t (h c) -> p t h c", c=32)
                    dve.wait_ge(s["maxa"], m)
                    dve.wait_ge(s["maxb"], m)
                    if ok(-1):
                        dve.wait_ge(s["Mt"], at(b, j, -1)[2])
                    else:
                        dve.wait_ge(s_ms, N_MS)
                    dve.tensor_copy(slots[:, :, :, 24], negm[:, :, :]).then_inc(s["mhi"], 1)
                    dve.wait_ge(s["mhi"], m)
                    dve.tensor_tensor(slots[:, :, :, 25], negm[:, :, :], slots[:, :, :, 24].bitcast(F32),
                                      ALU.subtract).then_inc(s["mx"], 1)
                if j == 0 and nxt:
                    dve.wait_ge(s["xh"], b + 2)
                    if cur:
                        dve.wait_ge(s_xp, b * 32 + 32)
                    dve.tensor_tensor(xl, J[:, 0:256], xh.bitcast(F32), ALU.subtract).then_inc(s["xl"], 1)
                if ok(1):
                    dve.wait_ge(s["Mt"], m)
                    if ok(-1):
                        dve.wait_ge(s["ST1"], at(b, j, -1)[2])
                    dve.tensor_tensor(q4b[j1 % 2], S0[:, 0:256], q4[j1].bitcast(F32), ALU.add)\
                        .then_inc(s["q4b"], 1)
                if ok(-1):
                    _, j9, m9 = at(b, j, -1)
                    view = X[:, 256:512].rearrange("p (t h c) -> p t h c", t=2, c=32)
                    dve.wait_ge(s["T"], m9)
                    if ok(-2):
                        dve.wait_ge(s["nm"], at(b, j, -2)[2])
                    dve.reciprocal(rden[:, :, :], view[:, :, :, HD]).then_inc(s["rc"], 1)
                if ok(4):
                    _, j4, m4 = at(b, j, 4)
                    dve.wait_ge(s["hi"], m4 * 2)
                    if ok(0):
                        dve.wait_ge(s["q4b"], at(b, j, 0)[2])
                        dve.wait_ge(s["S0"], at(b, j, 0)[2])
                        wait_kz(dve, b, j, 0)
                    dve.tensor_tensor(qk4[j4], J, hi4[:, :].bitcast(F32), ALU.subtract).then_inc(s["k4"], 1)
                if ok(-1):
                    dve.wait_ge(s["rc"], m9)
                    if j == 1 and prev:
                        dve.wait_ge(s["tT"], b)
                    dve.tensor_tensor(on[:, :, 32 * j9:32 * j9 + 32].rearrange("p t (h d) -> p t h d", h=4),
                                      view[:, :, :, 0:HD], rden[:, :, :].unsqueeze(3).to_broadcast([128, 2, 4, HD]),
                                      ALU.mult).then_inc(s["nm"], 1)

            pass_a(dve, body)

            cnt = [0]

            def rt(ins):
                cnt[0] += 1
                ins.then_inc(s["rt"], 1)
                dve.wait_ge(s["rt"], cnt[0])

            n = ROUTED

            def over(ap):
                return ap.unsqueeze(1).to_broadcast([128, n, TILES])

            dve.wait_ge(s["lg"], NB)
            rt(dve.tensor_copy(sel_r[:, 0:n, :],
                               const[0:16, C_SEL:C_ALL].unsqueeze(2).to_broadcast([16, n, 128])))
            rt(dve.tensor_tensor(r_a[:, 0:n, :], logit[:, 0:n, :],
                                 rb[:, 0:n].unsqueeze(2).to_broadcast([128, n, TILES]), ALU.add))
            rt(dve.tensor_reduce(r_s[:, 0, :], r_a[:, 0:n, :].rearrange("p e t -> p t e"), AX.X, ALU.max))
            rt(dve.tensor_tensor(r_b[:, 0:n, :], r_a[:, 0:n, :], over(r_s[:, 0, :]), ALU.subtract))
            dve.wait_ge(s["rx"], 1)
            rt(dve.tensor_reduce(r_s[:, 1, :], r_a[:, 0:n, :].rearrange("p e t -> p t e"), AX.X, ALU.add))
            rt(dve.reciprocal(r_s[:, 2, :], r_s[:, 1, :]))
            rt(dve.tensor_tensor(r_a[:, 0:n, :], r_a[:, 0:n, :], over(r_s[:, 2, :]), ALU.mult))
            for e in range(n):
                rt(dve.memset(r_b[:, e, :], float(n - 1 - e)))
            for d in range(1, n):
                rt(dve.tensor_tensor(r_c[:, 0:n - d, :], r_a[:, 0:n - d, :], r_a[:, d:n, :], ALU.is_ge))
                rt(dve.tensor_tensor(r_b[:, d:n, :], r_b[:, d:n, :], r_c[:, 0:n - d, :], ALU.add))
                rt(dve.tensor_tensor(r_b[:, 0:n - d, :], r_b[:, 0:n - d, :], r_c[:, 0:n - d, :], ALU.subtract))
            rt(dve.tensor_scalar(r_c[:, 0:n, :], r_b[:, 0:n, :], 1.5, None, ALU.is_lt))
            rt(dve.tensor_tensor(r_c[:, 0:n, :], r_c[:, 0:n, :], r_a[:, 0:n, :], ALU.mult))
            rt(dve.tensor_reduce(r_s[:, 0, :], r_c[:, 0:n, :].rearrange("p e t -> p t e"), AX.X, ALU.add))
            rt(dve.reciprocal(r_s[:, 1, :], r_s[:, 0, :]))
            rt(dve.tensor_tensor(r_b[:, 0:n, :], r_c[:, 0:n, :], over(r_s[:, 1, :]), ALU.mult))
            dve.wait_ge(s_ms, N_MS)
            w_te = r_b[:, 0:n, :].rearrange("p e t -> p t e")
            rt(dve.tensor_copy(whl[:, :, 0:n].bitcast(F32R), w_te))
            rt(dve.tensor_tensor(whl[:, :, 8:8 + n], w_te, whl[:, :, 0:n], ALU.subtract))

            dve.sem_inc(s["ob"], 1)

            def tile(c, u, ok):
                t = c * TPX + u
                e, i = u // 3, u % 3
                if ok(0) and u == 0:
                    if ok(-TPX):
                        dve.wait_ge(s["wT"], c)
                    dve.tensor_copy(wst[:, :, :], whl[:, bass.ds(c * TPC, TPC), :]).then_inc(s["wc"], 1)
                    dve.wait_ge(s["ohc"], c + 1)
                    dve.tensor_tensor(ol, o_all[:, bass.ds(c * CH, CH)], oh.bitcast(F32),
                                      ALU.subtract).then_inc(s["olc"], 1)
                if ok(0):
                    r = ROWS[i]
                    dve.wait_ge(s["s"], t + 1)
                    dve.wait_ge(s["U"], t + 1)
                    if ok(-2):
                        dve.wait_ge(s["hh"], t - 1)
                        split_ready(dve, c, u, -2)
                    dve.tensor_tensor(hf[u % 2][0:r, :], U[u % 2][0:r, :], s_b[u % 2][0:r, :], ALU.mult)\
                        .then_inc(s["mul"], 1)
                if ok(-1) and tl(c, u, -1)[2] != 0:
                    v = tl(c, u, -1)[3]
                    r = ROWS[v % 3]
                    dve.wait_ge(s["hh"], t)
                    dve.tensor_tensor(hl[v % 3][0:r, :], hf[v % 2][0:r, :], hh[v % 3][0:r, :].bitcast(F32),
                                      ALU.subtract).then_inc(s["hlD"], 1)
                if u == 5 and ok(-TPX):
                    dve.wait_ge(s["F"], c)
                    dve.wait_ge(s["out"], c * 16)
                    dve.tensor_tensor(ob, FT.rearrange("p (t e) -> p t e", t=TPC),
                                      x_sb[:, bass.ds((c - 1) * TPC, TPC), :], ALU.add).then_inc(s["ob"], 1)
                if ok(-3) and i == 2:
                    cc, ye, _, _ = tl(c, u, -3)
                    dve.wait_ge(s["dn"], t - 2)
                    if ye == 0:
                        if ok(-TPX):
                            dve.wait_ge(s["F"], cc)
                        dve.tensor_copy(acc, Y[0]).then_inc(s["yr"], 1)
                    else:
                        dve.wait_ge(s["wbc"], cc * ROUTED + ye)
                        if ok(-6) and ye > 1 or ok(-TPX):
                            dve.wait_ge(s["add"], cc * ROUTED + (ye - 1))
                        dve.tensor_tensor(yt, Y[ye % 2], wb[ye % 2], ALU.mult).then_inc(s["yr"], 1)

            pass_b(dve, tile)


def kernel(**inputs):
    import concourse.bacc as bacc
    from concourse.bass_utils import run_bass_kernel_spmd

    f = {k.split("_", 1)[1]: np.asarray(v) for k, v in inputs.items()}
    gate = np.concatenate([f["ffn_sg"][None], f["ffn_rg"]])
    up = np.concatenate([f["ffn_su"][None], f["ffn_ru"]])
    down = np.concatenate([f["ffn_sd"][None], f["ffn_rd"]])
    down = np.pad(down, ((0, 0), (0, 0), (0, 3 * 128 - INNER)))
    down = down.reshape(EXP, EMB, 3, 128).transpose(3, 0, 2, 1).reshape(128, EXP, 3 * EMB)
    w = np.concatenate([gate.transpose(2, 0, 1), up.transpose(2, 0, 1), down], axis=2)
    small = np.concatenate([f["attn_in_proj_weight"].T, f["attn_out_proj_weight"].T,
                            np.pad(f["ffn_wr"], ((0, 1), (0, 0))).T], axis=1)
    arrays = {
        "x": np.ascontiguousarray(f["attn_query"]),
        "small": np.ascontiguousarray(small),
        "rb": np.pad(f["ffn_rb"], (0, 1)),
        "w": np.ascontiguousarray(w.reshape(128, EXP * WE)),
        "consts": constants(),
    }
    nc = bacc.Bacc("TRN2", target_bir_lowering=False, num_devices=1)
    aps = [nc.dram_tensor(k, a.shape, F32, kind="ExternalInput").ap() for k, a in arrays.items()]
    out = nc.dram_tensor("out", (NB, SEQ, EMB), F32, kind="ExternalOutput").ap()
    build(nc, *aps, out)
    return run_bass_kernel_spmd(nc, [arrays], core_ids=[0]).results[0]["out"]
```

```python
from contextlib import ExitStack

import numpy as np

import concourse.bass as bass
from concourse import mybir

F32 = mybir.dt.float32
F32R = mybir.dt.float32r
BF16 = mybir.dt.bfloat16
ALU = mybir.AluOpType
ACT = mybir.ActivationFunctionType
AX = mybir.AxisListType

NB, SEQ, EMB = 16, 256, 128
HEADS, HD = 16, 8
QUADS = 4
NQ = NB * QUADS
TILES = NB * SEQ // 128
TPC = 4
CH = TPC * 128
NC = TILES // TPC
EXP, INNER = 8, 352
ROUTED = EXP - 1
TPX = EXP * INNER // 128
WT = 3 * 128
PIECE = TPX * WT // NB
N_MS = 5
N_PREP = 6
R_MAX = 96
QUARTERS = [(-2, 1), (-2, 3), (-1, 1)]
NEG = -1e30
SCALE = float(HD) ** -0.5
EPS = 1e-5
C_ID, C_MASK, C_COL, C_ALL = 0, 128, 256, 260
S_IN, S_V, S_R, S_OUT, S_ALL = 0, 256, 384, 392, 520


def constants():
    c = np.zeros((128, C_ALL), np.float32)
    p = np.arange(128)
    c[:, C_ID:C_ID + 128] = np.eye(128)
    c[:, C_MASK:C_MASK + 128] = np.where(p[:, None] >= p[None, :], 0.0, NEG)
    for h in range(4):
        c[:R_MAX, C_COL + h] = p[:R_MAX] % 32 // HD == h
        c[R_MAX + 2 * h:R_MAX + 2 * h + 2, C_COL + h] = 1.0
    return c


def experts_of(v):
    return tuple((128 * v + np.arange(128)) // INNER)


PLAIN = INNER // 128
FIRST = [v for v in range(PLAIN, TPX) if v == PLAIN or experts_of(v) != experts_of(v - 1)]
NP = len(FIRST)
PAT = [sum(f <= v for f in FIRST) - 1 for v in range(TPX)]
LAST = [max(v for v in range(TPX) if PAT[v] == p) for p in range(NP)]
WPC = TPX - PLAIN


def runs_of(v):
    e = experts_of(v)
    starts = [i for i in range(128) if i == 0 or e[i] != e[i - 1]]
    return [(a, z - a, int(e[a] - 1) % 8) for a, z in zip(starts, starts[1:] + [128])]


NWB = 3
LOADS = [sum(len(runs_of(v)) for v in FIRST[k::NWB]) for k in range(NWB)]
PREP = 14


def build(nc, x_d, small_d, rb_d, w_d, const_d, out_d):
    with ExitStack() as ctx:
        def sb(name, shape, dt=F32):
            return ctx.enter_context(nc.sbuf_tensor("sb_" + name, shape, dt))

        def sem(name):
            return ctx.enter_context(nc.semaphore(name))

        x_sb = sb("x_sb", [128, TILES, 128])
        xh_all = sb("xh_all", [128, NB * SEQ], F32R)
        xl_all = sb("xl_all", [128, NB * SEQ], F32R)
        o_all = sb("o_all", [128, NB * SEQ])
        wh_all = sb("wh_all", [128, TPX * WT], F32R)
        wl_all = sb("wl_all", [128, TPX * WT], F32R)
        const = sb("const", [128, C_ALL])
        ident_r = sb("ident_r", [128, 128], F32R)
        small = sb("small", [128, S_ALL])
        small_h = sb("small_h", [128, S_ALL], F32R)
        small_l = sb("small_l", [128, S_ALL], F32R)
        rb = sb("rb", [128, 8])
        logit = sb("logit", [128, 8, TILES])
        wtok = sb("wtok", [128, TILES, 8])
        wrow_d = nc.dram_tensor("wrow", (NC * 8, CH), F32).ap()
        ident = const[:, C_ID:C_ID + 128]

        work = sb("work", [128, 4096])
        ring = sb("ring", [128, 3072], F32R)
        P = [work[:, 1536 * k:1536 * k + 1536] for k in range(2)]
        v_sb = work[:, 3072:4096].rearrange("p (s h c) -> p s h c", s=2, h=HEADS)
        qk4 = [ring[:, 512 * k:512 * k + 512] for k in range(4)]
        q4 = [qk4[k][:, 0:256] for k in range(4)]
        k4 = [qk4[k][:, 256:512] for k in range(4)]
        q4b = [ring[:, 2048 + 256 * k:2304 + 256 * k] for k in range(2)]
        xsh = ring[:, 2560:2816]
        xsl = ring[:, 2816:3072]
        kz = [sb(f"kz{k}", [128, 4, 256], F32R) for k in range(4)]
        mexp = [sb(f"mexp{k}", [128, 2, 128], F32R) for k in range(2)]
        negm = sb("negm", [128, 2, 4])
        qk_h = sb("qk_h", [128, 512], F32R)
        qk_l = sb("qk_l", [128, 512], F32R)
        qk_f = sb("qk_f", [128, 512])
        x_f = sb("x_f", [128, 256])
        qk_d = nc.dram_tensor("qk", (NB * 3 * 128, 512), F32).ap()
        ot = sb("ot", [128, 256])
        vt = sb("vt", [128, 256])[:, :]
        on = sb("on", [128, 2, 128])
        rden = sb("rden", [128, 2, 4])
        xn = sb("xn", [128, 2, 128])
        mask_b = sb("mask_b", [128, 128], BF16)
        ident_b = sb("ident_b", [128, 128], BF16)
        stats = sb("stats", [128, TILES, 6])
        mv = sb("mv", [128, TILES, 2])
        rstd = sb("rstd", [128, TILES])
        std = sb("std", [128, TILES])
        eps = sb("eps", [128, 1])
        warm = sb("warm", [128, 3])
        stage = sb("stage", [128, PIECE])
        s_b = [work[:, 512 * k:512 * k + 512] for k in range(2)]
        hf = [work[:, 1024 + 512 * k:1536 + 512 * k] for k in range(2)]
        wb = [work[:, 2048 + 512 * k:2560 + 512 * k] for k in range(2)] + [ring[:, 2048:2560].bitcast(F32)]
        uw = [work[:, 3072 + 512 * k:3584 + 512 * k] for k in range(2)]
        acc = sb("acc", [128, CH])[:, :]
        ob = stage[:, 0:CH].rearrange("p (t e) -> p t e", t=TPC)
        hh = [ring[:, 1024 * k:1024 * k + 512] for k in range(2)]
        hl = [ring[:, 1024 * k + 512:1024 * k + 1024] for k in range(2)]
        oh, ol = [kz[0][:, 2 * k:2 * k + 2, :].rearrange("p a b -> p (a b)") for k in range(2)]
        wst = sb("wst", [128, TPC, 8])
        wtc = qk_h[0:8, :].bitcast(F32)
        r_a, r_b = [acc[:, 256 * k:256 * k + 256].rearrange("p (e t) -> p e t", t=TILES) for k in range(2)]
        r_c = xn[:, :, :].rearrange("p a (e t) -> p (a e) t", t=TILES)
        r_s = stats[:, :, :].rearrange("p a b -> p (a b)").rearrange("p (e t) -> p e t", t=TILES)

        ps = ctx.enter_context(nc.psum_tensor("ps", [128, 8, 512], F32))
        S0, J, X = ps[:, 0, :], ps[:, 6, :], ps[:, 7, :]
        S1 = ps[:, 1:3, :]
        T0 = ps[:, 3:5, :].rearrange("p b c -> p (b c)")
        T1 = ps[:, 5, :]
        G, U, Y = [ps[:, 0, :], ps[:, 1, :]], [ps[:, 2, :], ps[:, 3, :]], ps[:, 4, :]
        FT, WR = ps[:, 7, :], ps[0:8, 6, :]

        s_in = [sem(f"s_in{k}") for k in range(4)]
        s_sml = sem("s_sml")
        s_cst = sem("s_cst")
        s_prep = sem("s_prep")
        s_std = sem("s_std")
        s_ms = sem("s_ms")
        names = ("proj qh ql kza kzd S1 S0 maxa maxb mhi mx Mt q4b ST0 ST1 ea eb sel PV OT T rc nm "
                 "xn xT xh xl V va lg tT oT wcp wsp wld "
                 "rs idb var0 var G U s uw mul hh hl dn yr ohc olc wc wT wtc F ob out rt rx turnP turnS vt")
        s = {n: sem("s_" + n) for n in names.split()}
        s_qk = [sem(f"s_qk{k}") for k in range(4)]
        s_qd = sem("s_qd")
        s_wr = sem("s_wr")
        s_wb = [sem(f"s_wb{k}") for k in range(NWB)]
        s_xs = sem("s_xs")

        x_v = x_d.rearrange("b (s p) e -> p (b s) e", p=128)
        out_v = out_d.rearrange("b (s p) e -> p (b s) e", p=128)

        def steps(eng, body, groups, per, ahead, behind):
            total = groups * per
            last = groups - (ahead + per - 1) // per

            def peeled(a, z):
                for n in range(a, z):
                    body(n // per, n % per, lambda off, n=n: 0 <= n + off < total)

            peeled(-ahead, per)
            with eng.Fori(1, last) as g:
                for k in range(per):
                    body(g, k, lambda off: True)
            peeled(last * per, total + behind)

        def pass_a(eng, body):
            steps(eng, body, NB, QUADS, 8, 2)

        def pass_b(eng, body):
            steps(eng, body, NC, TPX, PREP, 6)

        def wb_loaded(c, p):
            k = p % NWB
            return c * (16 * LOADS[k]) + 16 * sum(len(runs_of(v)) for v in FIRST[k:p + 1:NWB])

        def at(b, j, off):
            bb, jj = b + (j + off) // 4, (j + off) % 4
            return bb, jj, bb * 4 + (jj + 1)

        def build_kz(eng, b, j, ok, heads, event):
            bb, j3, m = at(b, j, 3)
            eng.wait_ge(s_qk[j3], bb * 48 + 48)
            if not ok(-1):
                eng.wait_ge(s_prep, N_PREP)
            if ok(-1):
                eng.wait_ge(s["ST1"], at(b, j, -1)[2])
            for h in heads:
                mask = const[:, C_COL + h:C_COL + h + 1]
                if eng is nc.scalar:
                    last = eng.activation(kz[j3][:, h, :], k4[j3], ACT.Copy, scale=mask)
                else:
                    last = eng.tensor_scalar(kz[j3][:, h, :], k4[j3].bitcast(F32), mask, None, ALU.mult)
            last.then_inc(s[event], 1)

        def has(b):
            return 0 <= b < NB if isinstance(b, int) else True

        def tl(c, u, off):
            return c + (u + off) // TPX, (u + off) % TPX

        block = ctx.enter_context(nc.Block())

        @block.sync
        def _(sp):
            for k in range(4):
                sp.dma_start(x_sb[:, 8 * k:8 * k + 8, :], x_v[:, 8 * k:8 * k + 8, :]).then_inc(s_in[k], 16)
                if k == 0:
                    sp.dma_start(small[:, :], small_d).then_inc(s_sml, 16)
                    sp.dma_start(const[:, :], const_d).then_inc(s_cst, 16)
                    sp.dma_start(rb[:, :], rb_d.partition_broadcast(128)).then_inc(s_cst, 16)

            def body(b, j, ok):
                if ok(4):
                    bb, j4, _ = at(b, j, 4)
                    waits = [(s_qd, bb * 80 + 80)]
                    if ok(0):
                        m = at(b, j, 0)[2]
                        waits += [(s["q4b"], m), (s["kza"], m), (s["kzd"], m)]
                    else:
                        waits += [(s_ms, N_MS)]
                    for ready, value in waits:
                        sp.wait_ge(ready, value)
                        sp.sem_inc(s["turnS"], 1)
                    for r in range(3):
                        sp.dma_start(qk4[j4][32 * r:32 * r + 32, :].bitcast(F32),
                                     qk_d[bass.ds(bb * 384 + (128 * r + 32 * j4), 32), :]).then_inc(s_qk[j4], 16)
                if j == 3 and has(b + 2):
                    sp.wait_ge(s["ql"], b + 3)
                    sp.sem_inc(s["turnS"], 1)
                    for r, q, k in ((0, qk_h, qk_h), (1, qk_l, qk_h), (2, qk_h, qk_l)):
                        rows = bass.ds((b + 2) * 384 + 128 * r, 128)
                        for a, z, src in ((0, 512, q),) if q is k else ((0, 256, q), (256, 512, k)):
                            sp.dma_start(qk_d[rows, a:z], src[:, a:z].bitcast(F32)).then_inc(s_qd, 16)
                if j == 0 and has(b + 1):
                    sp.wait_ge(s["xl"], b + 2)
                    if has(b):
                        sp.wait_ge(s["V"], b + 1)
                    cols = bass.ds((b + 1) * SEQ, SEQ)
                    sp.dma_start(xsh.bitcast(F32), xh_all[:, cols].bitcast(F32)).then_inc(s_xs, 16)
                    sp.dma_start(xsl.bitcast(F32), xl_all[:, cols].bitcast(F32)).then_inc(s_xs, 16)
                if j == 0 and has(b):
                    if not isinstance(b, int) or b > 0:
                        sp.wait_ge(s["wsp"], b)
                    sp.dma_start(stage[:, :], w_d[:, bass.ds(b * PIECE, PIECE)]).then_inc(s["wld"], 16)

            pass_a(sp, body)

            def rows(c):
                sp.wait_ge(s["wtc"], c + 1)
                sp.sem_inc(s["turnS"], 1)
                sp.dma_start(wrow_d[bass.ds(c * 8, 8), :], wtc).then_inc(s_wr, 16)
                sp.wait_ge(s_wr, c * 16 + 16)
                sp.sem_inc(s["turnS"], 1)

            def broadcast(c, p):
                if p >= NWB:
                    sp.wait_ge(s["uw"], c * WPC + (LAST[p - NWB] - PLAIN + 1))
                elif not isinstance(c, int) or c > 0:
                    q = max(q for q in range(NP) if q % NWB == p)
                    sp.wait_ge(s["uw"], (c - 1) * WPC + (LAST[q] - PLAIN + 1))
                sp.sem_inc(s["turnS"], 1)
                for a, n, row in runs_of(FIRST[p]):
                    src = wrow_d[bass.ds(c * 8 + row, 1), :].rearrange("a t -> (a t)")
                    sp.dma_start(wb[p % NWB][a:a + n, :], src.partition_broadcast(n)).then_inc(s_wb[p % NWB], 16)

            def out_chunk(c):
                sp.wait_ge(s["ob"], c + 1)
                sp.sem_inc(s["turnS"], 1)
                sp.dma_start(out_v[:, bass.ds(c * TPC, TPC), :], ob).then_inc(s["out"], 16)

            def weights_and_out(c, before):
                rows(c)
                for p in range(NP):
                    broadcast(c, p)
                    if p == NP // 2 and before:
                        out_chunk(c - 1)

            sp.wait_ge(s["nm"], NQ)
            weights_and_out(0, False)
            with sp.Fori(1, NC) as c:
                weights_and_out(c, True)
            out_chunk(NC - 1)
            sp.wait_ge(s["out"], NC * 16)

        @block.gpsimd
        def _(pool):
            for buf in mexp:
                pool.memset(buf[:, :, :].bitcast(F32), 0.0).then_inc(s_ms, 1)
            pool.memset(v_sb[:, :, :, :], 0.0).then_inc(s_ms, 1)
            pool.wait_ge(s_ms, N_MS - 2)
            pool.memset(v_sb[:, :, :, HD:HD + 1], 1.0).then_inc(s_ms, 1)
            pool.memset(wtok[:, :, 7:8], 1.0).then_inc(s_ms, 1)

            def body(b, j, ok):
                if j == 1 and has(b + 2):
                    pool.wait_ge(s["xh"], b + 3)
                    pool.sem_inc(s["turnP"], 1)
                    cols = bass.ds((b + 2) * SEQ, SEQ)
                    pool.tensor_tensor(xl_all[:, cols], x_f[:, :], xh_all[:, cols].bitcast(F32),
                                       ALU.subtract).then_inc(s["xl"], 1)
                if j == 0 and has(b):
                    pool.wait_ge(s["vt"], b + 1)
                    if ok(-1):
                        pool.wait_ge(s["PV"], at(b, j, -1)[2])
                    else:
                        pool.wait_ge(s_ms, N_MS)
                    pool.sem_inc(s["turnP"], 1)
                    pool.tensor_copy(v_sb[:, :, :, 0:HD], vt.rearrange("p (s h d) -> p s h d", s=2, h=HEADS))\
                        .then_inc(s["va"], 1)
                if ok(0):
                    _, j0, m = at(b, j, 0)
                    for ev, o in (("ea", P[j0 % 2][:, 0:1024].rearrange("p (h q) -> p h q", h=4)[:, :, 0:128]),
                                  ("eb", P[j0 % 2][:, 1024:1536].rearrange("p (h q) -> p h q", h=4))):
                        pool.wait_ge(s[ev], m)
                        pool.sem_inc(s["turnP"], 1)
                        pool.affine_select(out=o, in_=o, compare_op=ALU.is_ge, fill=0.0, base=0,
                                           pattern=[[0, 4], [1, 128]], channel_multiplier=-1)\
                            .then_inc(s["sel"], 1)
                if j == 2 and has(b + 2):
                    pool.wait_ge(s["qh"], b + 3)
                    if has(b + 1):
                        pool.wait_ge(s_qd, b * 80 + 160)
                    pool.tensor_tensor(qk_l[:, :], qk_f[:, :], qk_h[:, :].bitcast(F32),
                                       ALU.subtract).then_inc(s["ql"], 1)
                if j == 1 and has(b):
                    cols = bass.ds(b * PIECE, PIECE)
                    pool.wait_ge(s["wld"], b * 16 + 16)
                    pool.tensor_copy(wh_all[:, cols], stage[:, :]).then_inc(s["wcp"], 1)
                if j == 3 and has(b):
                    cols = bass.ds(b * PIECE, PIECE)
                    pool.wait_ge(s["wcp"], b + 1)
                    pool.tensor_tensor(wl_all[:, cols], stage[:, :], wh_all[:, cols].bitcast(F32),
                                       ALU.subtract).then_inc(s["wsp"], 1)

            pass_a(pool, body)

            def tile(c, u, ok):
                t = c * TPX + u
                if ok(-1):
                    pool.wait_ge(s["hh"], t)
                    if ok(-3):
                        pool.wait_ge(s["dn"], t - 2)
                    pool.tensor_tensor(hl[(u - 1) % 2], hf[(u - 1) % 2], hh[(u - 1) % 2].bitcast(F32),
                                       ALU.subtract).then_inc(s["hl"], 1)

            pass_b(pool, tile)

        @block.scalar
        def _(act):
            def deviations(k):
                act.wait_ge(s["var0"], 1)
                act.wait_ge(s["var"], 2 * k + 2)
                act.activation(std[:, 8 * k:8 * k + 8], mv[:, 8 * k:8 * k + 8, 1], ACT.Sqrt, bias=eps[:, 0:1])\
                    .then_inc(s_std, 1)

            def load_table(k, function):
                act.activation(warm[:, k:k + 1], eps[:, :], function)

            act.wait_ge(s["var0"], 1)
            load_table(0, ACT.Sqrt)
            deviations(0)

            def body(b, j, ok):
                if ok(0):
                    _, j0, m = at(b, j, 0)
                    act.wait_ge(s["ST0"], m)
                    if ok(-2):
                        act.wait_ge(s["PV"], at(b, j, -2)[2])
                    act.activation(P[j0 % 2][:, 0:1024], T0, ACT.Exp, scale=SCALE).then_inc(s["ea"], 1)
                    act.wait_ge(s["ST1"], m)
                    act.activation(P[j0 % 2][:, 1024:1536], T1, ACT.Exp, scale=SCALE).then_inc(s["eb"], 1)
                    if not ok(1):
                        load_table(2, ACT.Silu)
                if j == 2 and has(b + 2):
                    act.wait_ge(s["proj"], b + 3)
                    if has(b + 1):
                        act.wait_ge(s_qd, b * 80 + 160)
                        act.wait_ge(s["ql"], b + 2)
                    act.activation(qk_h[:, :], J, ACT.Copy)
                    act.activation(qk_f[:, :], J, ACT.Copy).then_inc(s["qh"], 1)
                if j == 1 and has(b - 1):
                    act.wait_ge(s["tT"], b)
                    act.activation(o_all[:, bass.ds((b - 1) * SEQ, SEQ)], T1[:, 0:256], ACT.Copy)\
                        .then_inc(s["oT"], 1)
                if j == 0 and has(b + 2):
                    act.wait_ge(s["xT"], b + 3)
                    if has(b + 1):
                        act.wait_ge(s["xl"], b + 2)
                    act.activation(xh_all[:, bass.ds((b + 2) * SEQ, SEQ)], T1[:, 256:512], ACT.Copy)
                    act.activation(x_f[:, :], T1[:, 256:512], ACT.Copy).then_inc(s["xh"], 1)
                if ok(-1):
                    act.wait_ge(s["PV"], at(b, j, -1)[2])
                    if ok(-2):
                        act.wait_ge(s["nm"], at(b, j, -2)[2])
                    act.activation(ot[:, :], X[:, 0:256], ACT.Copy).then_inc(s["OT"], 1)
                if j == 3 and has(b + 1):
                    act.wait_ge(s["V"], b + 2)
                    if has(b):
                        act.wait_ge(s["va"], b + 1)
                    both = T1[:, 0:272].rearrange("p (t c) -> p t c", t=2)
                    act.activation(vt.rearrange("p (t c) -> p t c", t=2), both[:, :, 0:128], ACT.Copy)\
                        .then_inc(s["vt"], 1)
                    act.activation(logit[:, :, bass.ds((b + 1) * 2, 2)],
                                   both[:, :, 128:136].rearrange("p t e -> p e t"), ACT.Copy).then_inc(s["lg"], 1)
                if ok(3):
                    build_kz(act, b, j, ok, (0, 1, 2), "kza")
                if isinstance(b, int) and (b, j) in QUARTERS:
                    deviations(QUARTERS.index((b, j)) + 1)
                    if (b, j) == QUARTERS[-1]:
                        load_table(1, ACT.Exp)
                if isinstance(b, int) and (b, j) == (NB - 1, 1):
                    act.wait_ge(s["rt"], 3)
                    act.activation(r_a[:, 0:ROUTED, :], r_b[:, 0:ROUTED, :], ACT.Exp).then_inc(s["rx"], 1)

            pass_a(act, body)
            act.wait_ge(s["oT"], NB)

            def tile(c, u, ok):
                t = c * TPX + u
                if u == 2 and ok(-3):
                    act.wait_ge(s["dn"], c * TPX)
                    if ok(-2 * TPX):
                        act.wait_ge(s["F"], c - 1)
                    act.activation(acc, Y, ACT.Copy).then_inc(s["yr"], 1)
                if ok(-1):
                    act.wait_ge(s["mul"], t)
                    if ok(-3):
                        act.wait_ge(s["dn"], t - 2)
                    act.activation(hh[(u - 1) % 2], hf[(u - 1) % 2], ACT.Copy).then_inc(s["hh"], 1)
                if ok(0):
                    act.wait_ge(s["G"], t + 1)
                    if ok(-2):
                        act.wait_ge(s["mul"], t - 1)
                    act.activation(s_b[u % 2], G[u % 2], ACT.Silu).then_inc(s["s"], 1)
                if u == TPX - PREP and ok(PREP):
                    act.wait_ge(s["wT"], c + 2)
                    if ok(0):
                        act.wait_ge(s_wr, c * 16 + 16)
                    else:
                        act.wait_ge(s_qd, NB * 80)
                    act.activation(wtc, WR, ACT.Copy).then_inc(s["wtc"], 1)
                if ok(0) and u == 0:
                    if ok(-TPX):
                        act.wait_ge(s["dn"], (c - 1) * TPX + 1)
                    act.activation(oh, o_all[:, bass.ds(c * CH, CH)], ACT.Copy).then_inc(s["ohc"], 1)

            pass_b(act, tile)

        @block.tensor
        def _(pe):
            def mm3(out, wh, wl, xh_, xl_, start, stop):
                pe.matmul(out, wh, xh_, start=start, stop=False, skip_group_check=True)
                pe.matmul(out, wh, xl_, start=False, stop=False, skip_group_check=True)
                return pe.matmul(out, wl, xh_, start=False, stop=stop, skip_group_check=True)

            pe.wait_ge(s_prep, N_PREP)
            pe.wait_ge(s["idb"], 1)
            pe.wait_ge(s_ms, N_MS)

            def body(b, j, ok):
                if ok(1):
                    _, j1, m = at(b, j, 1)
                    if ok(0):
                        pe.wait_ge(s["q4b"], at(b, j, 0)[2])
                    pe.matmul(S0, q4[j1][:, 0:128], kz[j1][:, :, 0:128], start=True, stop=False,
                              skip_group_check=True)
                    last = pe.matmul(S0, ident_b[:, :], mask_b[:, :].unsqueeze(1).to_broadcast([128, 4, 128]),
                                     start=False, stop=True, skip_group_check=True)
                    last.then_inc(s["S0"], 1)
                if ok(0):
                    _, j0, m = at(b, j, 0)
                    z = kz[j0]
                    if not ok(1):
                        pe.wait_ge(s["q4b"], m)
                    if ok(-1):
                        pe.wait_ge(s["ea"], at(b, j, -1)[2])
                    for h in range(4):
                        last = pe.matmul(T0[:, 256 * h:256 * h + 256], z[:, h, 0:128], q4b[j0 % 2],
                                         start=True, stop=True)
                    last.then_inc(s["ST0"], 1)
                    if ok(-1):
                        pe.wait_ge(s["eb"], at(b, j, -1)[2])
                    if j == 0:
                        pe.wait_ge(s["lg"], b + 1)
                    if j == 1 and has(b + 2):
                        pe.wait_ge(s["xh"], b + 3)
                    if j == 2 and has(b - 1):
                        pe.wait_ge(s["oT"], b)
                    for h in range(4):
                        last = pe.matmul(T1[:, 128 * h:128 * h + 128], z[:, h, 128:256],
                                         q4b[j0 % 2][:, 128:256], start=True, stop=True)
                    last.then_inc(s["ST1"], 1)
                if ok(-1):
                    bb, j9, m = at(b, j, -1)
                    pe.wait_ge(s["sel"], m * 2)
                    pe.wait_ge(s["va"], bb + 1)
                    if ok(-2):
                        pe.wait_ge(s["OT"], at(b, j, -2)[2])
                    if ok(-3):
                        pe.wait_ge(s["nm"], at(b, j, -3)[2])
                    for h in range(4):
                        pe.matmul(X[32 * h:32 * h + 32, 0:256], v_sb[:, 0, 4 * j9 + h, :],
                                  P[j9 % 2][:, 256 * h:256 * h + 256], start=True, stop=False,
                                  skip_group_check=True)
                    for h in range(4):
                        last = pe.matmul(X[32 * h:32 * h + 32, 128:256], v_sb[:, 1, 4 * j9 + h, :],
                                         P[j9 % 2][:, 1024 + 128 * h:1152 + 128 * h], start=False, stop=True,
                                         skip_group_check=True)
                    last.then_inc(s["PV"], 1)
                if ok(-2):
                    pe.wait_ge(s["OT"], at(b, j, -2)[2])
                    for t in range(2):
                        last = pe.transpose(X[:, 256 + 128 * t:384 + 128 * t], ot[:, 128 * t:128 * t + 128], ident)
                    last.then_inc(s["T"], 1)
                if ok(1):
                    pe.wait_ge(s["mx"], at(b, j, 1)[2])
                    for t in range(2):
                        last = pe.matmul(S0[:, 128 * t:128 * t + 128], mexp[(j + 1) % 2][:, t, :], ident_r[:, :],
                                         start=True, stop=True)
                    last.then_inc(s["Mt"], 1)
                if ok(2):
                    _, j2, m = at(b, j, 2)
                    pe.wait_ge(s["kza"], m)
                    pe.wait_ge(s["kzd"], m)
                    if ok(1):
                        pe.wait_ge(s["maxa"], at(b, j, 1)[2])
                    for g in range(2):
                        pe.matmul(S1[:, g, :], q4[j2][:, 128:256],
                                  kz[j2][:, 2 * g:2 * g + 2, :].rearrange("p h k -> p (h k)"),
                                  start=True, stop=False, skip_group_check=True)
                        diag = S1[:, g, :].rearrange("p (h k) -> p h k", h=2)[:, :, 128:256]
                        last = pe.matmul(diag, ident_b[:, :], mask_b[:, :].unsqueeze(1).to_broadcast([128, 2, 128]),
                                         start=False, stop=True, skip_group_check=True)
                    last.then_inc(s["S1"], 1)
                if ok(0):
                    pe.wait_ge(s["eb"], at(b, j, 0)[2])
                if j == 1 and has(b - 1):
                    pe.wait_ge(s["nm"], b * 4)
                    for t in range(2):
                        last = pe.transpose(T1[:, 128 * t:128 * t + 128], on[:, t, :], ident)
                    last.then_inc(s["tT"], 1)
                if j == 0 and has(b + 2):
                    pe.wait_ge(s["xn"], b + 3)
                    for t in range(2):
                        last = pe.transpose(T1[:, 256 + 128 * t:384 + 128 * t], xn[:, t, :], ident)
                    last.then_inc(s["xT"], 1)
                if j == 3 and has(b + 1):
                    pe.wait_ge(s_xs, b * 32 + 64)
                    if not ok(0):
                        pe.wait_ge(s["xl"], b + 3)
                    for t in range(2):
                        for k, (lh, w) in enumerate(((xsh, small_h), (xsl, small_h), (xsh, small_l))):
                            last = pe.matmul(T1[:, 136 * t:136 * t + 136], lh[:, 128 * t:128 * t + 128],
                                             w[:, S_V:S_R + 8], start=(t == 0 and k == 0), stop=(k == 2),
                                             skip_group_check=True)
                    last.then_inc(s["V"], 1)
                if j == 1 and has(b + 2):
                    pe.wait_ge(s["xh"], b + 3)
                    pe.wait_ge(s["xl"], b + 3)
                    if has(b + 1):
                        pe.wait_ge(s["qh"], b + 2)
                    cols = bass.ds((b + 2) * SEQ, SEQ)
                    for w in range(2):
                        o = S_IN + 128 * w
                        last = mm3(J[:, 256 * w:256 * w + 256], small_h[:, o:o + 128], small_l[:, o:o + 128],
                                   xh_all[:, cols], xl_all[:, cols], w == 0, w == 1)
                    last.then_inc(s["proj"], 1)

            pass_a(pe, body)
            pe.wait_ge(s["wsp"], NB)
            pe.wait_ge(s["q4b"], NQ)
            pe.wait_ge(s["ea"], NQ)
            pe.wait_ge(s["nm"], NQ)

            def tile(c, u, ok):
                t = c * TPX + u
                if ok(0):
                    if ok(-2):
                        pe.wait_ge(s["mul"], t - 1)
                    xs = [a[:, bass.ds(c * CH, CH)] for a in (xh_all, xl_all)]
                    for k, (o, ev) in ((1, (U[u % 2], "U")), (0, (G[u % 2], "G"))):
                        w0 = u * WT + 128 * k
                        mm3(o, wh_all[:, w0:w0 + 128], wl_all[:, w0:w0 + 128], *xs, True, True)\
                            .then_inc(s[ev], 1)
                if u == TPX - PREP and ok(PREP):
                    pe.wait_ge(s["wc"], c + 2)
                    if ok(0):
                        pe.wait_ge(s["wtc"], c + 1)
                    for k in range(TPC):
                        last = pe.transpose(WR[:, 128 * k:128 * k + 128], wst[:, k, :], ident)
                    last.then_inc(s["wT"], 1)
                if ok(-2):
                    cc, v = tl(c, u, -2)
                    if v == 0:
                        if ok(-TPX - 2):
                            pe.wait_ge(s["yr"], cc)
                        pe.wait_ge(s["ohc"], cc + 1)
                        pe.wait_ge(s["olc"], cc + 1)
                        mm3(Y, small_h[:, S_OUT:S_OUT + 128], small_l[:, S_OUT:S_OUT + 128],
                            oh, ol, True, False)
                    pe.wait_ge(s["hh"], t - 1)
                    pe.wait_ge(s["hl"], t - 1)
                    w0 = v * WT + 256
                    mm3(Y, wh_all[:, w0:w0 + 128], wl_all[:, w0:w0 + 128], hh[v % 2], hl[v % 2],
                        False, v == TPX - 1).then_inc(s["dn"], 1)
                if u == 4 and ok(-TPX):
                    pe.wait_ge(s["yr"], c)
                    if ok(-2 * TPX):
                        pe.wait_ge(s["ob"], c - 1)
                    for k in range(TPC):
                        last = pe.transpose(FT[:, 128 * k:128 * k + 128], acc[:, 128 * k:128 * k + 128], ident)
                    last.then_inc(s["F"], 1)

            pass_b(pe, tile)

        @block.vector
        def _(dve):
            chain = [0]

            def link(ins, wait=True):
                chain[0] += 1
                ins.then_inc(s_prep, 1)
                if wait:
                    dve.wait_ge(s_prep, chain[0])

            def statistics(k):
                dve.wait_ge(s_in[k], 16)
                for t in range(8 * k, 8 * k + 8):
                    last = dve.bn_stats(stats[:, t, :], x_sb[:, t, :])
                last.then_inc(s["var"], 1)
                dve.wait_ge(s["var"], 2 * k + 1)
                for t in range(8 * k, 8 * k + 8):
                    last = dve.bn_aggr(mv[:, t, :], stats[:, t, :])
                last.then_inc(s["var"], 1)

            def reciprocals(k):
                dve.wait_ge(s_std, k + 1)
                dve.reciprocal(rstd[:, 8 * k:8 * k + 8], std[:, 8 * k:8 * k + 8]).then_inc(s["rs"], 1)
                dve.wait_ge(s["rs"], k + 1)

            dve.memset(eps[:, :], EPS).then_inc(s["var0"], 1)
            behind = ring[R_MAX:128, 0:2048].rearrange("p (j w c) -> p j w c", j=4, w=2).bitcast(F32)
            link(dve.memset(behind[:, :, 0, :], 0.0))
            link(dve.memset(behind[:, :, 1, :], 1.0))
            statistics(0)
            dve.wait_ge(s_sml, 16)
            link(dve.tensor_copy(small_h[:, :], small[:, :]))
            link(dve.tensor_tensor(small_l[:, :], small[:, :], small_h[:, :].bitcast(F32), ALU.subtract))
            reciprocals(0)

            def layer_norm(b):
                if not isinstance(b, int) or b > 0:
                    dve.wait_ge(s["xT"], b)
                for t in range(2):
                    k = b * 2 + t
                    last = dve.tensor_scalar(xn[:, t, :], x_sb[:, bass.ds(k, 1), :].rearrange("p a e -> p (a e)"),
                                             mv[:, bass.ds(k, 1), 0], rstd[:, bass.ds(k, 1)],
                                             ALU.subtract, ALU.mult)
                last.then_inc(s["xn"], 1)

            dve.wait_ge(s_cst, 32)
            link(dve.tensor_copy(ident_r[:, :], ident), wait=False)
            link(dve.tensor_copy(mask_b[:, :], const[:, C_MASK:C_MASK + 128]), wait=False)
            dve.tensor_copy(ident_b[:, :], ident).then_inc(s["idb"], 1)
            assert chain[0] == N_PREP

            def routing():
                n = ROUTED
                cnt = 0

                def rt(ins):
                    nonlocal cnt
                    cnt += 1
                    ins.then_inc(s["rt"], 1)
                    dve.wait_ge(s["rt"], cnt)

                def over(ap):
                    return ap.unsqueeze(1).to_broadcast([128, n, TILES])

                dve.wait_ge(s["lg"], NB)
                dve.wait_ge(s["xT"], NB)
                rt(dve.tensor_tensor(r_a[:, 0:n, :], logit[:, 0:n, :],
                                     rb[:, 0:n].unsqueeze(2).to_broadcast([128, n, TILES]), ALU.add))
                rt(dve.tensor_reduce(r_s[:, 0, :], r_a[:, 0:n, :].rearrange("p e t -> p t e"), AX.X, ALU.max))
                rt(dve.tensor_tensor(r_b[:, 0:n, :], r_a[:, 0:n, :], over(r_s[:, 0, :]), ALU.subtract))
                yield
                dve.wait_ge(s["rx"], 1)
                for e in range(n):
                    ins = dve.memset(r_b[:, e, :], float(n - 1 - e))
                rt(ins)
                rt(dve.tensor_reduce(r_s[:, 1, :], r_a[:, 0:n, :].rearrange("p e t -> p t e"), AX.X, ALU.add))
                rt(dve.reciprocal(r_s[:, 2, :], r_s[:, 1, :]))
                rt(dve.tensor_tensor(r_a[:, 0:n, :], r_a[:, 0:n, :], over(r_s[:, 2, :]), ALU.mult))
                yield
                for d in range(1, n):
                    rt(dve.tensor_tensor(r_c[:, 0:n - d, :], r_a[:, 0:n - d, :], r_a[:, d:n, :], ALU.is_ge))
                    rt(dve.tensor_tensor(r_b[:, d:n, :], r_b[:, d:n, :], r_c[:, 0:n - d, :], ALU.add))
                    rt(dve.tensor_tensor(r_b[:, 0:n - d, :], r_b[:, 0:n - d, :], r_c[:, 0:n - d, :], ALU.subtract))
                    if d % 2 == 0:
                        yield
                rt(dve.tensor_scalar(r_c[:, 0:n, :], r_b[:, 0:n, :], 1.5, None, ALU.is_lt))
                rt(dve.tensor_tensor(r_c[:, 0:n, :], r_c[:, 0:n, :], r_a[:, 0:n, :], ALU.mult))
                rt(dve.tensor_reduce(r_s[:, 0, :], r_c[:, 0:n, :].rearrange("p e t -> p t e"), AX.X, ALU.add))
                rt(dve.reciprocal(r_s[:, 1, :], r_s[:, 0, :]))
                dve.wait_ge(s_ms, N_MS)
                rt(dve.tensor_tensor(wtok[:, :, 0:n].rearrange("p t e -> p e t"), r_c[:, 0:n, :],
                                     over(r_s[:, 1, :]), ALU.mult))
                yield

            route = routing()

            def body(b, j, ok):
                if ok(1):
                    _, j1, m = at(b, j, 1)
                    dve.wait_ge(s["S1"], m)
                    if ok(0):
                        dve.wait_ge(s["mx"], at(b, j, 0)[2])
                    dve.tensor_reduce(negm[:, 1, :], S1.rearrange("p g (h k) -> p (g h) k", h=2), AX.X,
                                      ALU.max, negate=True).then_inc(s["maxa"], 1)
                    dve.wait_ge(s["S0"], m)
                    dve.tensor_reduce(negm[:, 0, :], S0.rearrange("p (h k) -> p h k", h=4), AX.X,
                                      ALU.max, negate=True).then_inc(s["maxb"], 1)
                    slots = mexp[j1 % 2][:, :, R_MAX:R_MAX + 8].rearrange("p t (h c) -> p t h c", c=2)
                    dve.wait_ge(s["maxa"], m)
                    dve.wait_ge(s["maxb"], m)
                    if ok(-1):
                        dve.wait_ge(s["Mt"], at(b, j, -1)[2])
                    else:
                        dve.wait_ge(s_ms, N_MS)
                    dve.tensor_copy(slots[:, :, :, 0], negm[:, :, :]).then_inc(s["mhi"], 1)
                    dve.wait_ge(s["mhi"], m)
                    dve.tensor_tensor(slots[:, :, :, 1], negm[:, :, :], slots[:, :, :, 0].bitcast(F32),
                                      ALU.subtract).then_inc(s["mx"], 1)
                if ok(3):
                    build_kz(dve, b, j, ok, (3,), "kzd")
                if ok(-2):
                    _, j9, m9 = at(b, j, -2)
                    view = X[:, 256:512].rearrange("p (t h c) -> p t h c", t=2, c=32)
                    dve.wait_ge(s["T"], m9)
                    if ok(-3):
                        dve.wait_ge(s["nm"], at(b, j, -3)[2])
                    dve.reciprocal(rden[:, :, :], view[:, :, :, HD]).then_inc(s["rc"], 1)
                    dve.wait_ge(s["rc"], m9)
                    if j == 2 and has(b - 1):
                        dve.wait_ge(s["tT"], b)
                    dve.tensor_tensor(on[:, :, 32 * j9:32 * j9 + 32].rearrange("p t (h d) -> p t h d", h=4),
                                      view[:, :, :, 0:HD], rden[:, :, :].unsqueeze(3).to_broadcast([128, 2, 4, HD]),
                                      ALU.mult).then_inc(s["nm"], 1)
                if j == 0 and has(b + 2):
                    layer_norm(b + 2)
                if isinstance(b, int) and (b, j) in QUARTERS:
                    k = QUARTERS.index((b, j)) + 1
                    statistics(k)
                    reciprocals(k)
                if ok(1):
                    dve.wait_ge(s["Mt"], m)
                    if ok(-1):
                        dve.wait_ge(s["ST1"], at(b, j, -1)[2])
                    dve.tensor_tensor(q4b[j1 % 2], S0[:, 0:256], q4[j1].bitcast(F32), ALU.add)\
                        .then_inc(s["q4b"], 1)
                if isinstance(b, int) and b >= NB - 1:
                    next(route)

            pass_a(dve, body)

            def tile(c, u, ok):
                t = c * TPX + u
                if u == TPX - PREP and ok(PREP):
                    if ok(0):
                        dve.wait_ge(s["wT"], c + 1)
                    dve.tensor_copy(wst[:, :, :], wtok[:, bass.ds((c + 1) * TPC, TPC), :]).then_inc(s["wc"], 1)
                if ok(-1):
                    v = (u - 1) % TPX
                    dve.wait_ge(s["s"], t)
                    if v >= PLAIN:
                        up = uw[v % 2]
                        dve.wait_ge(s["uw"], tl(c, u, -1)[0] * WPC + (v - PLAIN + 1))
                    else:
                        up = U[v % 2]
                        dve.wait_ge(s["U"], t)
                    if ok(-3):
                        dve.wait_ge(s["hh"], t - 2)
                        dve.wait_ge(s["hl"], t - 2)
                    dve.tensor_tensor(hf[v % 2], up, s_b[v % 2], ALU.mult).then_inc(s["mul"], 1)
                if ok(0) and u >= PLAIN:
                    dve.wait_ge(s["U"], t + 1)
                    dve.wait_ge(s_wb[PAT[u] % NWB], wb_loaded(c, PAT[u]))
                    if ok(-2):
                        dve.wait_ge(s["mul"], t - 1)
                    dve.tensor_tensor(uw[u % 2], U[u % 2], wb[PAT[u] % NWB], ALU.mult).then_inc(s["uw"], 1)
                if ok(0) and u == 1:
                    dve.wait_ge(s["ohc"], c + 1)
                    if ok(-TPX):
                        dve.wait_ge(s["dn"], (c - 1) * TPX + 1)
                    dve.tensor_tensor(ol, o_all[:, bass.ds(c * CH, CH)], oh.bitcast(F32),
                                      ALU.subtract).then_inc(s["olc"], 1)
                if u == 5 and ok(-TPX):
                    dve.wait_ge(s["F"], c)
                    if ok(-2 * TPX):
                        dve.wait_ge(s["out"], (c - 1) * 16)
                    dve.tensor_tensor(ob, FT.rearrange("p (t e) -> p t e", t=TPC),
                                      x_sb[:, bass.ds((c - 1) * TPC, TPC), :], ALU.add).then_inc(s["ob"], 1)

            pass_b(dve, tile)


def kernel(**inputs):
    import concourse.bacc as bacc
    from concourse.bass_utils import run_bass_kernel_spmd

    f = {k.split("_", 1)[1]: np.asarray(v) for k, v in inputs.items()}
    gate = np.concatenate([f["ffn_sg"][None], f["ffn_rg"]]).reshape(TPX, 128, EMB).transpose(2, 0, 1)
    up = np.concatenate([f["ffn_su"][None], f["ffn_ru"]]).reshape(TPX, 128, EMB).transpose(2, 0, 1)
    down = np.concatenate([f["ffn_sd"][None], f["ffn_rd"]]).transpose(0, 2, 1).reshape(TPX, 128, EMB)
    w = np.concatenate([gate, up, down.transpose(1, 0, 2)], axis=2)
    small = np.concatenate([f["attn_in_proj_weight"].T, np.pad(f["ffn_wr"], ((0, 1), (0, 0))).T,
                            f["attn_out_proj_weight"].T], axis=1)
    arrays = {
        "x": np.ascontiguousarray(f["attn_query"]),
        "small": np.ascontiguousarray(small),
        "rb": np.pad(f["ffn_rb"], (0, 1)),
        "w": np.ascontiguousarray(w.reshape(128, TPX * WT)),
        "consts": constants(),
    }
    nc = bacc.Bacc("TRN2", target_bir_lowering=False, num_devices=1)
    aps = [nc.dram_tensor(k, a.shape, F32, kind="ExternalInput").ap() for k, a in arrays.items()]
    out = nc.dram_tensor("out", (NB, SEQ, EMB), F32, kind="ExternalOutput").ap()
    build(nc, *aps, out)
    return run_bass_kernel_spmd(nc, [arrays], core_ids=[0]).results[0]["out"]
```
